# Optimizing a Trainium2 kernel written in Bass

```python
import numpy as np
import jax
import jax.numpy as jnp

def _softmax(x, axis=-1):
    return jax.nn.softmax(x, axis=axis)
def _gelu(x):
    return jax.nn.gelu(x, approximate=True)
def _silu(x):
    return jax.nn.silu(x)
def _sigmoid(x):
    return jax.nn.sigmoid(x)
def _layernorm(x, axis=-1, eps=1e-5):
    m = jnp.mean(x, axis=axis, keepdims=True)
    v = jnp.var(x, axis=axis, keepdims=True)
    return (x - m) / jnp.sqrt(v + eps)
def _scatter_add(tgt, idx, src, axis=0):
    return tgt.at[idx].add(src)
def _segment_sum(src, seg, n):
    return jax.ops.segment_sum(src, seg, n)

kernel_name = 'mk_adj_ffn_d2_adj_256_ce8814'

def setup_inputs(seed: int = 0):
    np.random.seed(seed)
    _w = jnp.asarray
    def _rec_inputs():
        import jax
        import jax.numpy as jnp
        _gk = jax.random.key(seed)
        x = -0.0005207 + 1.001 * jax.random.normal(jax.random.fold_in(_gk, 1), (2708, 256), jnp.float32)
        _w = (1.0 + jnp.arange(2708, dtype=jnp.float32)) ** -0.5
        _w = _w / _w.mean()
        _pij = jnp.clip(0.00295421 * _w[:, None] * _w[None, :], 0.0, 1.0)
        _a = jax.random.uniform(jax.random.fold_in(_gk, 2), (2708, 2708)) < _pij
        _a = jnp.logical_or(_a, jnp.eye(2708, dtype=bool))
        _af = _a.astype(jnp.float32)
        adj = _af
        return x, adj
    x, adj = _rec_inputs()
    def _L0_gnn_setup():
        import jax, jax.numpy as jnp
        import numpy as np
        N, IN_F, OUT_F, H = (8192, 256, 64, 4)
        NEG_SLOPE = 0.2
        key = jax.random.key(seed)
        ks = jax.random.split(key, 8)
        inputs = jax.random.normal(ks[0], (N, IN_F), dtype=jnp.float32)
        adj = (jax.random.uniform(ks[1], (N, N)) < 0.05).astype(jnp.float32)
        idx = jnp.arange(N)
        adj = adj.at[idx, idx].set(1.0)
        stdv = 1.0 / np.sqrt(H * OUT_F)
        weight = jax.random.uniform(ks[2], (IN_F, H * OUT_F), minval=-stdv, maxval=stdv, dtype=jnp.float32)
        bias = jax.random.uniform(ks[3], (1, H * OUT_F), minval=-stdv, maxval=stdv, dtype=jnp.float32)
        weight_u = jax.random.uniform(ks[4], (H, OUT_F, 1), minval=-1.0, maxval=1.0, dtype=jnp.float32)
        weight_v = jax.random.uniform(ks[5], (H, OUT_F, 1), minval=-1.0, maxval=1.0, dtype=jnp.float32)
        stdp = 1.0 / np.sqrt(IN_F)
        proj_w = jax.random.uniform(ks[6], (H * OUT_F, IN_F), minval=-stdp, maxval=stdp, dtype=jnp.float32)
        proj_b = jax.random.uniform(ks[7], (H * OUT_F,), minval=-stdp, maxval=stdp, dtype=jnp.float32)
        return {'inputs': inputs, 'adj_mat': adj, 'weight': weight, 'weight_u': weight_u, 'weight_v': weight_v, 'bias': bias, 'proj_w': proj_w, 'proj_b': proj_b}
    _L0_gnn_all = _L0_gnn_setup()
    _L0_gnn_in = {k: v for k, v in _L0_gnn_all.items() if k in ('weight', 'weight_u', 'weight_v', 'bias', 'proj_w', 'proj_b', )}
    del _L0_gnn_all

    def _L0_ffn_setup():
        import jax, jax.numpy as jnp
        import numpy as np
        B, S, H, F, E, K = (8, 4096, 256, 512, 16, 2)
        EPS = 1e-05
        key = jax.random.key(seed)
        ks = jax.random.split(key, 9)
        sc = 0.02
        return {'x': jax.random.normal(ks[0], (B, S, H), dtype=jnp.float32), 'gate_w': jax.random.normal(ks[1], (H, E), dtype=jnp.float32) * sc, 'gate_b': jnp.zeros((E,), dtype=jnp.float32), 'w1': jax.random.normal(ks[2], (E, H, F), dtype=jnp.float32) * sc, 'b1': jnp.zeros((E, F), dtype=jnp.float32), 'w2': jax.random.normal(ks[3], (E, F, H), dtype=jnp.float32) * sc, 'b2': jnp.zeros((E, H), dtype=jnp.float32), 'gamma': jnp.ones((H,), dtype=jnp.float32), 'beta': jnp.zeros((H,), dtype=jnp.float32)}
    _L0_ffn_all = _L0_ffn_setup()
    _L0_ffn_in = {k: v for k, v in _L0_ffn_all.items() if k in ('gate_w', 'gate_b', 'w1', 'b1', 'w2', 'b2', 'gamma', 'beta', )}
    del _L0_ffn_all

    def _L1_gnn_setup():
        import jax, jax.numpy as jnp
        import numpy as np
        N = 8192
        DIM = 256
        HEADS = 4
        HD = DIM // HEADS
        SCALE = HD ** (-0.5)
        key = jax.random.key(seed)
        ks = jax.random.split(key, 8)
        x = jax.random.normal(ks[0], (N, DIM), dtype=jnp.float32)
        adj_matrix = jax.random.uniform(ks[1], (N, N), dtype=jnp.float32)
        attn_mask = jax.random.randint(ks[2], (N, N), 0, 2, dtype=jnp.int32)
        Wqkv = jax.random.normal(ks[3], (DIM, 3 * DIM), dtype=jnp.float32) * DIM ** (-0.5)
        bqkv = jnp.zeros((3 * DIM,), dtype=jnp.float32)
        Wout = jax.random.normal(ks[4], (DIM, DIM), dtype=jnp.float32) * DIM ** (-0.5)
        bout = jnp.zeros((DIM,), dtype=jnp.float32)
        graph_bias = jax.random.normal(ks[5], (1, 1, 1), dtype=jnp.float32) * 0.1
        return {'x': x, 'adj_matrix': adj_matrix, 'attn_mask': attn_mask, 'Wqkv': Wqkv, 'bqkv': bqkv, 'Wout': Wout, 'bout': bout, 'graph_bias': graph_bias}
    _L1_gnn_all = _L1_gnn_setup()
    _L1_gnn_in = {k: v for k, v in _L1_gnn_all.items() if k in ('Wqkv', 'bqkv', 'Wout', 'bout', 'graph_bias', )}
    del _L1_gnn_all

    def _L1_ffn_setup():
        import jax, jax.numpy as jnp
        import numpy as np
        C = 256
        EPS = 1e-05
        N_ITERS = 30

        def _layernorm(x, w, bias):
            mu = jnp.mean(x, axis=-1, keepdims=True)
            var = jnp.mean(jnp.square(x - mu), axis=-1, keepdims=True)
            return (x - mu) * jax.lax.rsqrt(var + EPS) * w + bias
        key = jax.random.key(seed)
        kx, kw, kb, klw, klb = jax.random.split(key, 5)
        x = jax.random.normal(kx, (8, 2048, C), dtype=jnp.float32)
        bound = 1.0 / np.sqrt(C)
        W = jax.random.uniform(kw, (C, C), minval=-bound, maxval=bound, dtype=jnp.float32)
        b = jax.random.uniform(kb, (C,), minval=-bound, maxval=bound, dtype=jnp.float32)
        ln_w = jnp.ones((C,), dtype=jnp.float32)
        ln_b = jnp.zeros((C,), dtype=jnp.float32)
        return {'x': x, 'ln_w': ln_w, 'ln_b': ln_b, 'W': W, 'b': b}
    _L1_ffn_all = _L1_ffn_setup()
    _L1_ffn_in = {k: v for k, v in _L1_ffn_all.items() if k in ('ln_w', 'ln_b', 'W', 'b', )}
    del _L1_ffn_all

    return {
        "x": x,
        "adj": adj,
        "L0_gnn_weight": _L0_gnn_in["weight"],
        "L0_gnn_weight_u": _L0_gnn_in["weight_u"],
        "L0_gnn_weight_v": _L0_gnn_in["weight_v"],
        "L0_gnn_bias": _L0_gnn_in["bias"],
        "L0_gnn_proj_w": _L0_gnn_in["proj_w"],
        "L0_gnn_proj_b": _L0_gnn_in["proj_b"],
        "L0_ffn_gate_w": _L0_ffn_in["gate_w"],
        "L0_ffn_gate_b": _L0_ffn_in["gate_b"],
        "L0_ffn_w1": _L0_ffn_in["w1"],
        "L0_ffn_b1": _L0_ffn_in["b1"],
        "L0_ffn_w2": _L0_ffn_in["w2"],
        "L0_ffn_b2": _L0_ffn_in["b2"],
        "L0_ffn_gamma": _L0_ffn_in["gamma"],
        "L0_ffn_beta": _L0_ffn_in["beta"],
        "L1_gnn_Wqkv": _L1_gnn_in["Wqkv"],
        "L1_gnn_bqkv": _L1_gnn_in["bqkv"],
        "L1_gnn_Wout": _L1_gnn_in["Wout"],
        "L1_gnn_bout": _L1_gnn_in["bout"],
        "L1_gnn_graph_bias": _L1_gnn_in["graph_bias"],
        "L1_ffn_ln_w": _L1_ffn_in["ln_w"],
        "L1_ffn_ln_b": _L1_ffn_in["ln_b"],
        "L1_ffn_W": _L1_ffn_in["W"],
        "L1_ffn_b": _L1_ffn_in["b"],
    }

def reference(x, adj, L0_gnn_weight, L0_gnn_weight_u, L0_gnn_weight_v, L0_gnn_bias, L0_gnn_proj_w, L0_gnn_proj_b, L0_ffn_gate_w, L0_ffn_gate_b, L0_ffn_w1, L0_ffn_b1, L0_ffn_w2, L0_ffn_b2, L0_ffn_gamma, L0_ffn_beta, L1_gnn_Wqkv, L1_gnn_bqkv, L1_gnn_Wout, L1_gnn_bout, L1_gnn_graph_bias, L1_ffn_ln_w, L1_ffn_ln_b, L1_ffn_W, L1_ffn_b):
    import jax
    import jax.numpy as jnp
    def _L0_gnn_ref(inputs, adj_mat, weight, weight_u, weight_v, bias, proj_w, proj_b):
        import jax, jax.numpy as jnp
        import numpy as np
        N, IN_F, OUT_F, H = (8192, 256, 64, 4)
        NEG_SLOPE = 0.2
        n = inputs.shape[0]
        support = (inputs @ weight).reshape(n, H, OUT_F).transpose(1, 0, 2)
        f1 = jnp.einsum('hno,ho->hn', support, weight_u[..., 0])
        f2 = jnp.einsum('hno,ho->hn', support, weight_v[..., 0])
        logits = f1[:, None, :] + f2[:, :, None]
        w = jax.nn.leaky_relu(logits, NEG_SLOPE)
        masked = w * adj_mat
        mask = adj_mat != 0.0
        neg = jnp.where(mask, masked, -jnp.inf)
        m = jnp.max(neg, axis=2, keepdims=True)
        m = jnp.where(jnp.isfinite(m), m, 0.0)
        e = jnp.where(mask, jnp.exp(neg - m), 0.0)
        denom = jnp.sum(e, axis=2, keepdims=True)
        attn = e / jnp.where(denom > 0, denom, 1.0)
        out = jnp.einsum('hnm,hmo->hno', attn, support)
        out = out.transpose(1, 0, 2).reshape(n, H * OUT_F)
        out = out + bias
        out = out + inputs @ proj_w.T + proj_b
        return out

    def _L0_ffn_ref(x, gate_w, gate_b, w1, b1, w2, b2, gamma, beta):
        import jax, jax.numpy as jnp
        import numpy as np
        B, S, H, F, E, K = (8, 4096, 256, 512, 16, 2)
        EPS = 1e-05
        gate_logits = x @ gate_w + gate_b
        topk_vals, topk_idx = jax.lax.top_k(gate_logits, K)
        topk_w = jax.nn.softmax(topk_vals, axis=-1)
        h = jax.nn.relu(jnp.einsum('bsh,ehf->bsef', x, w1) + b1)
        expert_out = jnp.einsum('bsef,efh->bseh', h, w2) + b2
        sel = jnp.take_along_axis(expert_out, topk_idx[:, :, :, None], axis=2)
        moe = jnp.sum(topk_w[..., None] * sel, axis=2)
        y = x + moe
        mu = jnp.mean(y, axis=-1, keepdims=True)
        var = jnp.var(y, axis=-1, keepdims=True)
        return (y - mu) / jnp.sqrt(var + EPS) * gamma + beta

    def _L1_gnn_ref(x, adj_matrix, attn_mask, Wqkv, bqkv, Wout, bout, graph_bias):
        import jax, jax.numpy as jnp
        import numpy as np
        N = 8192
        DIM = 256
        HEADS = 4
        HD = DIM // HEADS
        SCALE = HD ** (-0.5)
        n, d = x.shape
        qkv = x @ Wqkv + bqkv
        q, k, v = jnp.split(qkv, 3, axis=-1)

        def split_heads(t):
            return t.reshape(n, HEADS, HD).transpose(1, 0, 2)
        qh, kh, vh = (split_heads(q), split_heads(k), split_heads(v))
        scores = jnp.einsum('hnd,hmd->hnm', qh, kh) * SCALE
        scores = scores + graph_bias * adj_matrix[None, :, :]
        scores = jnp.where(attn_mask[None, :, :] == 0, jnp.float32(-1000000000.0), scores)
        attn = jax.nn.softmax(scores, axis=-1)
        out = jnp.einsum('hnm,hmd->hnd', attn, vh)
        out = out.transpose(1, 0, 2).reshape(n, d)
        return out @ Wout + bout

    def _L1_ffn_ref(x, ln_w, ln_b, W, b):
        import jax, jax.numpy as jnp
        import numpy as np
        C = 256
        EPS = 1e-05
        N_ITERS = 30

        def _layernorm(x, w, bias):
            mu = jnp.mean(x, axis=-1, keepdims=True)
            var = jnp.mean(jnp.square(x - mu), axis=-1, keepdims=True)
            return (x - mu) * jax.lax.rsqrt(var + EPS) * w + bias
        def step(h, _):
            h = h + 0.01 * jnp.tanh(h)
            h = h * jax.nn.sigmoid(h)
            h = _layernorm(h, ln_w, ln_b)
            h = jnp.einsum('bsc,dc->bsd', h, W) + b
            return (h, None)
        x, _ = jax.lax.scan(step, x, None, length=N_ITERS)
        return x

    x = x + _L0_gnn_ref(_layernorm(x, axis=-1), adj, L0_gnn_weight, L0_gnn_weight_u, L0_gnn_weight_v, L0_gnn_bias, L0_gnn_proj_w, L0_gnn_proj_b)
    x = x + _L0_ffn_ref((_layernorm(x, axis=-1))[None], L0_ffn_gate_w, L0_ffn_gate_b, L0_ffn_w1, L0_ffn_b1, L0_ffn_w2, L0_ffn_b2, L0_ffn_gamma, L0_ffn_beta)[0]
    x = x + _L1_gnn_ref(_layernorm(x, axis=-1), adj, adj, L1_gnn_Wqkv, L1_gnn_bqkv, L1_gnn_Wout, L1_gnn_bout, L1_gnn_graph_bias)
    x = x + _L1_ffn_ref((_layernorm(x, axis=-1))[None], L1_ffn_ln_w, L1_ffn_ln_b, L1_ffn_W, L1_ffn_b)[0]
    return x


_drawn_inputs = setup_inputs


def setup_inputs(seed=0):
    import zlib

    import numpy as np

    out = dict(_drawn_inputs(seed))
    spreads = {'L0_ffn_gate_b': (0.0, 0.1),
     'L0_ffn_b1': (0.0, 0.543),
     'L0_ffn_b2': (0.0, 0.1),
     'L0_ffn_gamma': (1.0, 0.2),
     'L0_ffn_beta': (0.0, 0.1),
     'L1_gnn_bqkv': (0.0, 0.1),
     'L1_gnn_bout': (0.0, 0.1),
     'L1_ffn_ln_w': (1.0, 0.2),
     'L1_ffn_ln_b': (0.0, 0.1)}
    factors = {}
    for name, (base, spread) in spreads.items():
        noise = np.random.default_rng([zlib.crc32(name.encode()), seed]).standard_normal(out[name].shape)
        drawn = base * np.exp(spread * noise) if base else spread * noise
        out[name] = jnp.asarray(drawn.astype(out[name].dtype))
    for name, factor in factors.items():
        out[name] = (out[name] * factor).astype(out[name].dtype)
    return out
```

```python
from contextlib import ExitStack

import concourse.bass as bass
from concourse import mybir

ALU = mybir.AluOpType
ACT = mybir.ActivationFunctionType
AX = mybir.AxisListType
F32 = mybir.dt.float32
F16 = mybir.dt.float16
BF16 = mybir.dt.bfloat16
U32 = mybir.dt.uint32
I32 = mybir.dt.int32

P = 128
N = 2708
D = 256
KD = D // P
NT = -(-N // P)
LAST = N - P
OVER = P * NT - N
H, HD = 4, 64
VW = HD + 1
NPAIR = NT // 2
GRP = 4
NG = -(-NT // GRP)
E, F, TOPK = 16, 512, 2
FB = F // P
XTILES = (TOPK * NT * P + E * (P - 1)) // P + 1
XTILES += XTILES % 2
ITERS = 30
EPS = 1e-5
SLOPE = 0.2
BIG = 3e38
FLOOR = -1e37
MASKED = -1e9


class Phase:

    def __init__(self, nc, name):
        self.nc, self.name, self.ctx = nc, name, ExitStack()
        self.counters = []

    def __enter__(self):
        self.ctx.__enter__()
        return self

    def __exit__(self, *a):
        done = self.ctx.__exit__(*a)
        self.nc.clear_and_free_semaphores(self.counters)
        self.nc.all_engine_barrier()
        return done

    def sb(self, name, shape, dt=F32):
        return self.ctx.enter_context(self.nc.sbuf_tensor(f"{self.name}_{name}", shape, dt))

    def ps(self, name, shape, dt=F32):
        return self.ctx.enter_context(self.nc.psum_tensor(f"{self.name}_{name}", shape, dt))

    def sem(self, name):
        self.counters.append(self.nc.alloc_semaphore(f"{self.name}_{name}"))
        return self.counters[-1]

    def sems(self, names):
        return [self.sem(n) for n in names.split()]

    def block(self):
        return self.ctx.enter_context(self.nc.Block())


def some(n):
    return not isinstance(n, int) or n > 0


def bcast_rows(ap, rows):
    return ap.rearrange("(a d) -> a d", a=1).to_broadcast([rows, ap.shape[0]])


def row_moments(dve, st, mom, s0, s1, chain, base):
    n = slice(s0, s1)
    even_m, even_q, odd_m, odd_q = (st[:, n, j] for j in (1, 2, 4, 5))
    dve.tensor_tensor(mom[:, 0, n], even_m, odd_m, ALU.add)
    dve.tensor_tensor(mom[:, 2, n], even_m, odd_m, ALU.subtract).then_inc(chain, 1)
    dve.tensor_tensor(mom[:, 3, n], even_q, odd_q, ALU.add).then_inc(chain, 1)
    dve.wait_ge(chain, base + 1)
    dve.scalar_tensor_tensor(mom[:, 4, n], mom[:, 2, n], 0.25, mom[:, 2, n],
                             ALU.mult, ALU.mult).then_inc(chain, 1)
    dve.wait_ge(chain, base + 3)
    return dve.scalar_tensor_tensor(mom[:, 1, n], mom[:, 3, n], 1.0 / D, mom[:, 4, n], ALU.mult, ALU.add)


def inverse_deviation(pool, mom, rs, neg_half, s0, s1, chain, base):
    n = slice(s0, s1)
    pool.tensor_scalar(rs[:, 2, n], mom[:, 1, n], EPS, None, ALU.add).then_inc(chain, 1)
    pool.tensor_scalar(rs[:, 3, n], mom[:, 0, n], -0.5, None, ALU.mult).then_inc(chain, 1)
    pool.wait_ge(chain, base + 1)
    pool.tensor_tensor(rs[:, 0, n], rs[:, 2, n], neg_half[:, n], ALU.pow).then_inc(chain, 1)
    pool.wait_ge(chain, base + 3)
    return pool.tensor_tensor(rs[:, 1, n], rs[:, 3, n], rs[:, 0, n], ALU.mult)



def standard_rows(eng, out, x, rs, t):
    return eng.tensor_scalar(out, x, rs[:, 0, bass.ds(t, 1)], rs[:, 1, bass.ds(t, 1)], ALU.mult, ALU.add)


def slot_pairs(eng, body):
    with eng.Fori(0, NPAIR - 1) as i:
        for b in range(2):
            body(i, b)
    for b in range(2):
        body(NPAIR - 1, b)


def slot_moments(dve, x, st, mom, stats, folded, moments):
    with dve.Fori(0, NT) as t:
        dve.bn_stats(st[:, bass.ds(t, 1), :], x[:, bass.ds(t, 1), :]).then_inc(stats, 1)
    dve.wait_ge(stats, NT)
    row_moments(dve, st, mom, 0, NT, folded, 0).then_inc(moments, 1)


def layer0_prepare(nc, io, keep):
    X, V, F1, F2, ident, neg_half = (keep[n] for n in ("X", "V", "F1", "F2", "ident", "neg_half"))
    with Phase(nc, "p0") as ph:
        w = ph.sb("w", [P, KD, D + H])
        pw = ph.sb("pw", [P, KD, D])
        pwt = ph.sb("pwt", [P, KD, KD, P])
        uv = ph.sb("uv", [P, 2, D])
        prod = ph.sb("prod", [P, 2, KD, D])
        wuv = ph.sb("wuv", [P, 2, KD, H])
        wub = ph.sb("wub", [P, KD, H, P])
        bias = ph.sb("bias", [P, 3, D])
        zeros = ph.sb("zeros", [P, D])
        ones = ph.sb("ones", [P, P])
        rows_kept = ph.sb("rows_kept", [P, 1])
        st = ph.sb("st", [P, NT, 6])
        mom = ph.sb("mom", [P, 5, NT])
        rs = ph.sb("rs", [P, 4, NT])
        xn = ph.sb("xn", [P, 2, D])
        xt = ph.sb("xt", [P, 2, KD, P])
        pt = ph.ps("pt", [P, 2, 512])
        pf = ph.ps("pf", [P, 2, 512])
        pv = ph.ps("pv", [P, 2, 512])
        pp = ph.ps("pp", [P, 2, 512])
        (x_in, w_in, cleared, consts, stats, moments, inv, pchain, folded, wub_done, pwt_ps, pwt_sb,
         bsum, xd_zero, prods, masked) = ph.sems(
            "x_in w_in cleared consts stats moments inv pchain folded wub_done pwt_ps pwt_sb "
            "bsum xd_zero prods masked")
        xn_done, turned, xt_done, f_mm, v_mm, p_mm, f_out, v_out, biased, x_out = (
            ph.sems(f"{n}0 {n}1") for n in
            "xn_done turned xt_done f_mm v_mm p_mm f_out v_out biased x_out".split())
        block = ph.block()

        @block.sync
        def _(sp):
            sp.dma_start(X[:, 0:NT - 1, :], io["x"][0:P * (NT - 1), :].rearrange("(t p) d -> p t d", p=P)
                         ).then_inc(x_in, 16)
            sp.dma_start(X[:, NT - 1, :], io["x"][LAST:N, :]).then_inc(x_in, 16)
            sp.dma_start(w[:, :, 0:D], io["L0_gnn_weight"].rearrange("(k p) o -> p k o", p=P)).then_inc(w_in, 16)
            sp.dma_start(pw[:, :, :], io["L0_gnn_proj_w"].rearrange("(k p) o -> p k o", p=P)).then_inc(w_in, 16)
            for j, name in enumerate(("L0_gnn_weight_u", "L0_gnn_weight_v")):
                sp.dma_start(uv[:, j, :], bcast_rows(io[name].rearrange("h o a -> (h o a)"), P)).then_inc(w_in, 16)
            sp.dma_start(bias[:, 0, :], io["L0_gnn_bias"].to_broadcast([P, D])).then_inc(w_in, 16)
            sp.dma_start(bias[:, 1, :], bcast_rows(io["L0_gnn_proj_b"], P)).then_inc(w_in, 16)
            sp.wait_ge(cleared, 2)
            sp.dma_start(keep["XD"].rearrange("(j p) d -> p j d", p=P),
                         zeros[:, :].rearrange("p (a d) -> p a d", a=1).to_broadcast([P, XTILES, D])
                         ).then_inc(xd_zero, 16)
            sp.wait_ge(xd_zero, 16)

        @block.gpsimd
        def _(pool):
            pool.memset(ident[:, :], 0.0).then_inc(cleared, 1)
            pool.memset(zeros[:, :], 0.0).then_inc(cleared, 1)
            pool.memset(rows_kept[:, :], 1.0).then_inc(cleared, 1)
            pool.memset(neg_half[:, :], -0.5).then_inc(cleared, 1)
            pool.wait_ge(cleared, 4)
            pool.affine_select(out=ident[:, :], in_=ident[:, :], compare_op=ALU.not_equal, fill=1.0, base=0,
                               pattern=[[-1, P]], channel_multiplier=1).then_inc(consts, 1)
            pool.affine_select(out=rows_kept[:, :], in_=rows_kept[:, :], compare_op=ALU.is_ge, fill=0.0,
                               base=-OVER, pattern=[[0, 1]], channel_multiplier=1).then_inc(consts, 1)
            pool.wait_ge(w_in, 96)
            pool.tensor_tensor(bias[:, 2, :], bias[:, 0, :], bias[:, 1, :], ALU.add).then_inc(bsum, 1)
            pool.wait_ge(moments, 1)
            inverse_deviation(pool, mom, rs, neg_half, 0, NT, pchain, 0).then_inc(inv, 1)
            pool.wait_ge(inv, 1)
            pool.wait_ge(bsum, 1)

            def normal(i, b):
                t = i * 2 + b
                if some(i):
                    pool.wait_ge(turned[b], i)
                xs = X[:, bass.ds(t, 1), :]
                standard_rows(pool, xn[:, b:b + 1, :], xs, rs, t).then_inc(xn_done[b], 1)
                pool.wait_ge(xn_done[b], i + 1)
                pool.tensor_tensor(xs, xs, bias[:, 2:3, :], ALU.add).then_inc(biased[b], 1)
            for t in range(NT):
                normal(t // 2, t % 2)

        @block.vector
        def _(dve):
            dve.memset(ones[:, :], 1.0).then_inc(prods, 1)
            dve.memset(V[:, :, :, HD:VW], 1.0)
            dve.wait_ge(x_in, 32)
            slot_moments(dve, X, st, mom, stats, folded, moments)
            dve.wait_ge(w_in, 96)
            for j in range(2):
                for k in range(KD):
                    dve.tensor_tensor(prod[:, j, k, :], w[:, k, 0:D], uv[:, j, :], ALU.mult).then_inc(prods, 1)
            dve.wait_ge(prods, 5)
            for j in range(2):
                dve.tensor_reduce(wuv[:, j, :, :], prod[:, j, :, :].rearrange("p k (h o) -> p k h o", h=H),
                                  AX.X, ALU.add).then_inc(prods, 1)
            dve.wait_ge(prods, 7)
            dve.tensor_copy(w[:, :, D:D + H], wuv[:, 1, :, :]).then_inc(wub_done, 1)
            for k in range(KD):
                for h in range(H):
                    dve.tensor_scalar(wub[:, k, h, :], ones[:, :], wuv[:, 0, k, h:h + 1], None,
                                      ALU.mult).then_inc(wub_done, 1)

            def results(i, b):
                t = i * 2 + b
                dve.wait_ge(v_mm[b], i + 1)
                dve.tensor_copy(V[:, bass.ds(t, 1), :, 0:HD],
                                pv[:, b:b + 1, 0:D].rearrange("p a (h o) -> p a h o", h=H)).then_inc(v_out[b], 1)
                dve.tensor_copy(F2[:, 0, bass.ds(t, 1), :], pv[:, b:b + 1, D:D + H]).then_inc(v_out[b], 1)
                dve.wait_ge(p_mm[b], i + 1)
                dve.wait_ge(biased[b], i + 1)
                xs = X[:, bass.ds(t, 1), :]
                dve.tensor_tensor(xs, pp[:, b:b + 1, 0:D], xs, ALU.add).then_inc(x_out[b], 1)
            slot_pairs(dve, results)
            for b in range(2):
                dve.wait_ge(v_out[b], 2 * NPAIR)
            dve.wait_ge(consts, 2)
            dve.tensor_scalar(V[:, NT - 1, :, :], V[:, NT - 1, :, :], rows_kept[:, :], None, ALU.mult).then_inc(masked, 1)
            dve.tensor_scalar(F2[:, 1, :, :], F2[:, 0, :, :], SLOPE, None, ALU.mult).then_inc(masked, 1)
            dve.wait_ge(masked, 2)

        @block.tensor
        def _(pe):
            pe.wait_ge(w_in, 96)
            pe.wait_ge(consts, 1)
            for k in range(KD):
                for j in range(KD):
                    mm = pe.transpose(pf[:, 0, (k * KD + j) * P:(k * KD + j + 1) * P],
                                      pw[:, j, k * P:(k + 1) * P], ident[:, :])
            mm.then_inc(pwt_ps, 1)
            pe.wait_ge(pwt_sb, 1)
            pe.wait_ge(wub_done, 1 + KD * H)

            def turn(i, b):
                pe.wait_ge(xn_done[b], i + 1)
                if some(i):
                    pe.wait_ge(xt_done[b], i)
                for k in range(KD):
                    mm = pe.transpose(pt[:, b, k * P:(k + 1) * P], xn[:, b, k * P:(k + 1) * P], ident[:, :])
                mm.then_inc(turned[b], 1)

            def product(i, b):
                pe.wait_ge(xt_done[b], i + 1)
                if some(i):
                    pe.wait_ge(f_out[b], i)
                if some(i * 2):
                    pe.wait_ge(v_out[b], i * 2)
                if some(i):
                    pe.wait_ge(x_out[b], i)
                for h in range(H):
                    for k in range(KD):
                        mm = pe.matmul(pf[:, b, h * P:(h + 1) * P], wub[:, k, h, :], xt[:, b, k, :],
                                       start=(k == 0), stop=(k == KD - 1))
                mm.then_inc(f_mm[b], 1)
                for k in range(KD):
                    mm = pe.matmul(pv[:, b, 0:D + H], xt[:, b, k, :], w[:, k, :],
                                   start=(k == 0), stop=(k == KD - 1))
                mm.then_inc(v_mm[b], 1)
                for k in range(KD):
                    mm = pe.matmul(pp[:, b, 0:D], xt[:, b, k, :], pwt[:, k, :, :],
                                   start=(k == 0), stop=(k == KD - 1))
                mm.then_inc(p_mm[b], 1)

            turn(0, 0)
            def pair(i):
                turn(i, 1)
                product(i, 0)
                turn(i + 1, 0)
                product(i, 1)
            pair(0)
            with pe.Fori(1, NPAIR - 1) as i:
                pair(i)
            turn(NPAIR - 1, 1)
            product(NPAIR - 1, 0)
            product(NPAIR - 1, 1)

        @block.scalar
        def _(act):
            act.wait_ge(pwt_ps, 1)
            act.copy(pwt[:, :, :, :], pf[:, 0, :]).then_inc(pwt_sb, 1)
            act.wait_ge(pwt_sb, 1)

            def turned_out(i, b):
                act.wait_ge(turned[b], i + 1)
                act.copy(xt[:, b, :, :], pt[:, b, 0:D]).then_inc(xt_done[b], 1)

            def f1_out(i, b):
                act.wait_ge(f_mm[b], i + 1)
                col = LAST if isinstance(i, int) and i * 2 + b == NT - 1 else (i * 2 + b) * P
                act.copy(F1[:, :, bass.ds(col, P)],
                         pf[:, b, :].rearrange("p (h n) -> p h n", h=H)).then_inc(f_out[b], 1)

            turned_out(0, 0)
            with act.Fori(0, NPAIR - 1) as i:
                turned_out(i, 1)
                f1_out(i, 0)
                turned_out(i + 1, 0)
                f1_out(i, 1)
            turned_out(NPAIR - 1, 1)
            f1_out(NPAIR - 1, 0)
            act.wait_ge(f_out[0], NPAIR)
            f1_out(NPAIR - 1, 1)


def later(unit, k):
    i, b, h = unit
    n = b * H + h + k
    i = i + n // (2 * H)
    if isinstance(i, int) and not 0 <= i < NPAIR:
        return None
    return i, n % (2 * H) // H, n % H


def over_units(eng, step):
    def pair(i):
        for b in range(2):
            for h in range(H):
                step((i, b, h))
    pair(0)
    with eng.Fori(1, NPAIR - 1) as i:
        pair(i)
    pair(NPAIR - 1)


def layer0_attention(nc, io, keep):
    X, V, F1, F2, ident = (keep[n] for n in ("X", "V", "F1", "F2", "ident"))
    with Phase(nc, "a0") as ph:
        adj = ph.sb("adj", [P, 2, N])
        off = ph.sb("off", [P, 2, N])
        low = ph.sb("low", [P, N])
        lg = ph.sb("lg", [P, H, N])
        wt = ph.sb("wt", [P, NT, P])
        mx = ph.sb("mx", [P, H, 2])
        den = ph.sb("den", [P, 2, 2, H])
        res = ph.sb("res", [P, 2, H, HD])
        tp = ph.ps("tp", [P, NG, 512])
        po = ph.ps("po", [P, 2, 512])
        adj_in, off_done, heads_in, heads_out, d_ok, r_ok, n_ok = (
            ph.sems(f"{n}0 {n}1") for n in "adj_in off_done heads_in heads_out d_ok r_ok n_ok".split())
        low_done, lrelu, times, masked, neg_max, exp_done = (
            ph.sems(" ".join(f"{n}{h}" for h in range(H))) for n in
            "low_done lrelu times masked neg_max exp_done".split())
        turned = ph.sems(" ".join(f"turned{g}" for g in range(NG)))
        copied = ph.sems(" ".join(f"copied{g}" for g in range(NG)))
        block = ph.block()
        by_dve = (NG - 2, NG - 1)

        def tiles(unit):
            i, b, h = unit
            return i * 2 + (b + 1)

        def units(unit):
            i, b, h = unit
            return i * (2 * H) + (b * H + h + 1)

        def copies(eng, copy, unit, groups):
            for g in groups:
                n = min(GRP, NT - GRP * g)
                eng.wait_ge(turned[g], units(unit))
                copy(wt[:, GRP * g:GRP * g + n, :], tp[:, g, 0:n * P]).then_inc(copied[g], 1)

        @block.sync
        def _(sp):
            for b in range(2):
                sp.dma_start(adj[:, b, :], io["adj"][b * P:(b + 1) * P, :]).then_inc(adj_in[b], 16)
            with sp.Fori(1, NPAIR - 1) as i:
                for b in range(2):
                    sp.wait_ge(masked[H - 1], i * 2 + (b - 1))
                    sp.dma_start(adj[:, b, :], io["adj"][bass.ds((i * 2 + b) * P, P), :]).then_inc(adj_in[b], 16)
            for b in range(2):
                sp.wait_ge(masked[H - 1], (NPAIR - 1) * 2 + b - 1)
                row = (NT - 2) * P if b == 0 else LAST
                sp.dma_start(adj[:, b, :], io["adj"][row:row + P, :]).then_inc(adj_in[b], 16)

        @block.gpsimd
        def _(pool):
            def off_tile(i, b):
                pool.wait_ge(adj_in[b], i * 16 + 16)
                pool.nop(nofuse=True)
                pool.tensor_scalar(off[:, b, :], adj[:, b, :], 0.0, -BIG, ALU.is_equal,
                                   ALU.mult).then_inc(off_done[b], 1)

            def step(unit):
                i, b, h = unit
                pool.wait_ge(lrelu[h], tiles(unit))
                if h == 0:
                    pool.wait_ge(adj_in[b], i * 16 + 16)
                pool.nop(nofuse=True)
                pool.tensor_tensor(lg[:, h, :], lg[:, h, :], adj[:, b, :], ALU.mult).then_inc(times[h], 1)
                if h == 1 and later(unit, H):
                    off_tile(*later(unit, H)[:2])
            off_tile(0, 0)
            over_units(pool, step)

        @block.scalar
        def _(act):
            def low_part(unit):
                i, b, h = unit
                if later(unit, -1):
                    act.wait_ge(lrelu[later(unit, -1)[2]], tiles(later(unit, -1)))
                act.activation(low[:, :], F1[:, h, :], ACT.Identity, scale=SLOPE,
                               bias=F2[:, 1, bass.ds(i * 2 + b, 1), h]).then_inc(low_done[h], 1)

            def exp_part(unit):
                h = unit[2]
                act.wait_ge(neg_max[h], tiles(unit))
                act.activation(lg[:, h, :], lg[:, h, :], ACT.Exp, bias=mx[:, h, 1:2]).then_inc(exp_done[h], 1)

            def step(unit):
                before, after = later(unit, -1), later(unit, 2)
                if before:
                    exp_part(before)
                if after:
                    low_part(after)
                if before:
                    copies(act, act.copy, before, range(NG - len(by_dve)))
            low_part((0, 0, 0))
            low_part((0, 0, 1))
            over_units(act, step)
            last = (NPAIR - 1, 1, H - 1)
            exp_part(last)
            copies(act, act.copy, last, range(NG - len(by_dve)))

        @block.vector
        def _(dve):
            def leaky(unit):
                i, b, h = unit
                dve.wait_ge(low_done[h], tiles(unit))
                dve.scalar_tensor_tensor(lg[:, h, :], F1[:, h, :], F2[:, 0, bass.ds(i * 2 + b, 1), h],
                                         low[:, :], ALU.add, ALU.max).then_inc(lrelu[h], 1)

            def mask(unit):
                i, b, h = unit
                if h == 0:
                    dve.wait_ge(off_done[b], i + 1)
                dve.wait_ge(times[h], tiles(unit))
                dve.nop(nofuse=True)
                dve.tensor_tensor_reduce(lg[:, h, :], lg[:, h, :], off[:, b, :], 1.0, -BIG, ALU.add, ALU.max,
                                         mx[:, h, 0:1]).then_inc(masked[h], 1)
                dve.wait_ge(masked[h], tiles(unit))
                dve.tensor_scalar(mx[:, h, 1:2], mx[:, h, 0:1], FLOOR, -1.0, ALU.max,
                                  ALU.mult).then_inc(neg_max[h], 1)

            def finish(i, b):
                sums = po[:, b, 0:H * VW].rearrange("p (h v) -> p h v", h=H)
                dve.wait_ge(heads_in[b], i + 1)
                dve.tensor_scalar(den[:, b, 0, :], sums[:, :, HD], 1e-30, None, ALU.max).then_inc(d_ok[b], 1)
                dve.wait_ge(d_ok[b], i + 1)
                dve.reciprocal(den[:, b, 1, :], den[:, b, 0, :]).then_inc(r_ok[b], 1)
                dve.wait_ge(r_ok[b], i + 1)
                dve.tensor_tensor(res[:, b, :, :], sums[:, :, 0:HD],
                                  den[:, b, 1, :].rearrange("p (h a) -> p h a", a=1).to_broadcast([P, H, HD]),
                                  ALU.mult).then_inc(n_ok[b], 1)
                dve.wait_ge(n_ok[b], i + 1)
                xs = X[:, bass.ds(i * 2 + b, 1), :]
                dve.tensor_tensor(xs, xs, res[:, b:b + 1, :, :].rearrange("p a h o -> p a (h o)"),
                                  ALU.add).then_inc(heads_out[b], 1)

            def step(unit):
                if later(unit, 1):
                    leaky(later(unit, 1))
                mask(unit)
                if later(unit, -1):
                    copies(dve, dve.tensor_copy, later(unit, -1), by_dve)
                if unit[2] == 1 and later(unit, -H):
                    finish(*later(unit, -H)[:2])
            leaky((0, 0, 0))
            over_units(dve, step)
            copies(dve, dve.tensor_copy, (NPAIR - 1, 1, H - 1), by_dve)
            finish(NPAIR - 1, 1)

        @block.tensor
        def _(pe):
            def step(unit):
                i, b, h = unit
                pe.wait_ge(exp_done[h], tiles(unit))
                for g in range(NG):
                    for j in range(GRP * g, min(GRP * g + GRP, NT)):
                        col = min(j * P, LAST)
                        mm = pe.transpose(tp[:, g, (j % GRP) * P:(j % GRP + 1) * P],
                                          lg[:, h, col:col + P], ident[:, :])
                    mm.then_inc(turned[g], 1)
                if h == 0 and some(i):
                    pe.wait_ge(heads_out[b], i)
                for g in range(NG):
                    pe.wait_ge(copied[g], units(unit))
                    for j in range(GRP * g, min(GRP * g + GRP, NT)):
                        mm = pe.matmul(po[:, b, h * VW:(h + 1) * VW], wt[:, j, :], V[:, j, h, :],
                                       start=(j == 0), stop=(j == NT - 1))
                if h == H - 1:
                    mm.then_inc(heads_in[b], 1)
            over_units(pe, step)


def layer1_prepare(nc, io, keep, layer1):
    X, V, ident, neg_half = (keep[n] for n in ("X", "V", "ident", "neg_half"))
    QT, KH, KL = (layer1[n] for n in ("QT", "KH", "KL"))
    with Phase(nc, "p1") as ph:
        wqkv = ph.sb("wqkv", [P, KD, 3 * D])
        wqk = ph.sb("wqk", [P, KD, 2, H, 2, HD])
        bqk = ph.sb("bqk", [P, 2, H])
        bv = ph.sb("bv", [P, D])
        rows_kept = ph.sb("rows_kept", [P, 1])
        st = ph.sb("st", [P, NT, 6])
        mom = ph.sb("mom", [P, 5, NT])
        rs = ph.sb("rs", [P, 4, NT])
        xn = ph.sb("xn", [P, 2, D])
        xt = ph.sb("xt", [P, 2, KD, P])
        full = ph.sb("full", [P, 2, 2, H, P])
        pt = ph.ps("pt", [P, 2, 512])
        pq = ph.ps("pq", [P, 2, 512])
        pk = ph.ps("pk", [P, 2, 512])
        pv = ph.ps("pv", [P, 2, 512])
        (w_in, b_in, scaled, kept0, kept, stats, moments, inv, pchain, folded, doubled, masked) = ph.sems(
            "w_in b_in scaled kept0 kept stats moments inv pchain folded doubled masked")
        xn_done, turned, xt_done, q_mm, k_mm, v_mm, q_full, k_full, high_done, low_done, v_out = (
            ph.sems(f"{n}0 {n}1") for n in
            "xn_done turned xt_done q_mm k_mm v_mm q_full k_full high_done low_done v_out".split())
        block = ph.block()

        @block.sync
        def _(sp):
            sp.dma_start(wqkv[:, :, :], io["L1_gnn_Wqkv"].rearrange("(k p) o -> p k o", p=P)).then_inc(w_in, 16)
            sp.dma_start(bv[:, :], bcast_rows(io["L1_gnn_bqkv"][2 * D:3 * D], P)).then_inc(b_in, 16)
            with nc.allow_non_contiguous_dma(reason="a bias column per head"):
                for r in range(2):
                    sp.dma_start(bqk[r * HD:(r + 1) * HD, :, :],
                                 io["L1_gnn_bqkv"][0:2 * D].rearrange("(j h o) -> o j h", j=2, h=H)
                                 ).then_inc(b_in, 16)

        @block.gpsimd
        def _(pool):
            pool.memset(rows_kept[:, :], 1.0).then_inc(kept0, 1)
            pool.wait_ge(kept0, 1)
            pool.affine_select(out=rows_kept[:, :], in_=rows_kept[:, :], compare_op=ALU.is_ge, fill=0.0,
                               base=-OVER, pattern=[[0, 1]], channel_multiplier=1).then_inc(kept, 1)
            pool.wait_ge(w_in, 16)
            for j in range(2):
                for r in range(2):
                    for k in range(KD):
                        pool.tensor_copy(wqk[:, k, j, :, r, :], wqkv[:, k, j * D:(j + 1) * D].rearrange(
                            "p (h o) -> p h o", h=H)).then_inc(doubled, 1)
            pool.wait_ge(moments, 1)
            inverse_deviation(pool, mom, rs, neg_half, 0, NT, pchain, 0).then_inc(inv, 1)
            pool.wait_ge(inv, 1)

            def normal(i, b):
                if some(i):
                    pool.wait_ge(turned[b], i)
                standard_rows(pool, xn[:, b:b + 1, :], X[:, bass.ds(i * 2 + b, 1), :], rs,
                              i * 2 + b).then_inc(xn_done[b], 1)
            for t in range(NT):
                normal(t // 2, t % 2)

        @block.vector
        def _(dve):
            dve.memset(V[:, :, :, HD:VW], 1.0)
            slot_moments(dve, X, st, mom, stats, folded, moments)
            dve.wait_ge(b_in, 48)

            def results(i, b):
                t = i * 2 + b
                last = isinstance(i, int) and t == NT - 1
                col = LAST if last else t * P
                dve.wait_ge(q_full[b], i * H + H)
                dve.wait_ge(k_full[b], i * H + H)
                dve.tensor_copy(QT[:, :, bass.ds(t * P, P)], full[:, b, 0, :, :]).then_inc(high_done[b], 1)
                if last:
                    dve.wait_ge(low_done[0], 2 * NPAIR)
                dve.tensor_copy(KH[:, :, bass.ds(col, P)], full[:, b, 1, :, :]).then_inc(high_done[b], 1)
                dve.wait_ge(v_mm[b], i + 1)
                dve.tensor_tensor(V[:, bass.ds(t, 1), :, 0:HD],
                                  pv[:, b:b + 1, 0:D].rearrange("p a (h o) -> p a h o", h=H),
                                  bv[:, :].rearrange("p (a h o) -> p a h o", a=1, h=H),
                                  ALU.add).then_inc(v_out[b], 1)
                dve.wait_ge(high_done[b], i * 2 + 2)
                lows = slice(HD, P)
                dve.tensor_tensor(QT[lows, :, bass.ds(t * P, P)], full[lows, b, 0, :, :],
                                  QT[lows, :, bass.ds(t * P, P)], ALU.subtract).then_inc(low_done[b], 1)
                dve.tensor_tensor(KL[:, :, bass.ds(col, P)], full[:, b, 1, :, :], KH[:, :, bass.ds(col, P)],
                                  ALU.subtract).then_inc(low_done[b], 1)
            slot_pairs(dve, results)
            for b in range(2):
                dve.wait_ge(v_out[b], NPAIR)
            dve.wait_ge(kept, 1)
            dve.tensor_scalar(V[:, NT - 1, :, :], V[:, NT - 1, :, :], rows_kept[:, :], None,
                              ALU.mult).then_inc(masked, 1)
            dve.wait_ge(masked, 1)

        @block.scalar
        def _(act):
            act.wait_ge(b_in, 48)
            act.activation(bqk[:, 0, :], bqk[:, 0, :], ACT.Identity, scale=HD ** -0.5).then_inc(scaled, 1)
            act.wait_ge(scaled, 1)

            def turned_out(i, b):
                act.wait_ge(turned[b], i + 1)
                act.copy(xt[:, b, :, :], pt[:, b, 0:D]).then_inc(xt_done[b], 1)

            def full_out(i, b):
                if some(i * 2):
                    act.wait_ge(low_done[b], i * 2)
                for j, (done, mm, src, scale) in enumerate(((q_full, q_mm, pq, HD ** -0.5),
                                                            (k_full, k_mm, pk, 1.0))):
                    act.wait_ge(mm[b], i + 1)
                    for h in range(H):
                        act.activation(full[:, b, j, h, :], src[:, b, h * P:(h + 1) * P], ACT.Identity,
                                       scale=scale, bias=bqk[:, j, h:h + 1]).then_inc(done[b], 1)

            turned_out(0, 0)
            def pair(i):
                turned_out(i, 1)
                full_out(i, 0)
                turned_out(i + 1, 0)
                full_out(i, 1)
            pair(0)
            with act.Fori(1, NPAIR - 1) as i:
                pair(i)
            turned_out(NPAIR - 1, 1)
            full_out(NPAIR - 1, 0)
            full_out(NPAIR - 1, 1)

        @block.tensor
        def _(pe):
            pe.wait_ge(w_in, 16)
            pe.wait_ge(doubled, 8)

            def turn(i, b):
                pe.wait_ge(xn_done[b], i + 1)
                if some(i):
                    pe.wait_ge(xt_done[b], i)
                for k in range(KD):
                    mm = pe.transpose(pt[:, b, k * P:(k + 1) * P], xn[:, b, k * P:(k + 1) * P], ident[:, :])
                mm.then_inc(turned[b], 1)

            def product(i, b):
                pe.wait_ge(xt_done[b], i + 1)
                for j, (mm_done, out_done, dst) in enumerate(((q_mm, q_full, pq), (k_mm, k_full, pk))):
                    if some(i * H):
                        pe.wait_ge(out_done[b], i * H)
                    for h in range(H):
                        for k in range(KD):
                            mm = pe.matmul(dst[:, b, h * P:(h + 1) * P],
                                           wqk[:, k, j, h, :, :].rearrange("p r o -> p (r o)"),
                                           xt[:, b, k, :], start=(k == 0), stop=(k == KD - 1))
                    mm.then_inc(mm_done[b], 1)
                if some(i):
                    pe.wait_ge(v_out[b], i)
                for k in range(KD):
                    mm = pe.matmul(pv[:, b, 0:D], xt[:, b, k, :], wqkv[:, k, 2 * D:3 * D],
                                   start=(k == 0), stop=(k == KD - 1))
                mm.then_inc(v_mm[b], 1)

            turn(0, 0)
            def pair(i):
                turn(i, 1)
                product(i, 0)
                turn(i + 1, 0)
                product(i, 1)
            pair(0)
            with pe.Fori(1, NPAIR - 1) as i:
                pair(i)
            turn(NPAIR - 1, 1)
            product(NPAIR - 1, 0)
            product(NPAIR - 1, 1)


CHUNKS = [(c, min(1024, N - c)) for c in range(0, N, 1024)]
NC = len(CHUNKS)
TB = 3


def layer1_attention(nc, io, keep, layer1):
    V, ident = keep["V"], keep["ident"]
    QT, KH, KL = (layer1[n] for n in ("QT", "KH", "KL"))
    with Phase(nc, "a1") as ph:
        adj = ph.sb("adj", [P, 2, N])
        off = ph.sb("off", [P, N])
        gb = ph.sb("gb", [P, 1])
        sc = ph.sb("sc", [P, 2, N])
        wt = ph.sb("wt", [P, NT, P])
        mx = ph.sb("mx", [P, 2, NC + 1])
        den = ph.sb("den", [P, 2, H])
        res = ph.sb("res", [P, 2, H, HD])
        qk = ph.ps("qk", [P, 2, 1024])
        tp = ph.ps("tp", [P, TB, 512])
        po = ph.ps("po", [P, 512])
        (adj_in, off_done, scaled_adj, bias_done, neg_max, exp_done, r_ok, n_ok, stored, qk_done) = (ph.sems(f"{n}0 {n}1") for n in
              ("adj_in off_done scaled_adj bias_done neg_max exp_done r_ok n_ok stored qk_done"
               ).split())
        masked = [ph.sems(" ".join(f"masked{b}{c}" for c in range(NC))) for b in range(2)]
        turned = ph.sems(" ".join(f"turned{g}" for g in range(NG)))
        copied = ph.sems(" ".join(f"copied{g}" for g in range(NG)))
        heads_in, gb_in = ph.sems("heads_in gb_in")
        block = ph.block()
        by_dve = (1, 3, 5)
        by_act = (0, 2, 4)

        def units(unit):
            i, b, h = unit
            return i * (2 * H) + (b * H + h + 1)

        def parity(unit):
            i, b, h = unit
            return i * H + (b * (H // 2) + h // 2 + 1)

        def copies(eng, copy, unit, groups):
            for g in groups:
                n = min(GRP, NT - GRP * g)
                eng.wait_ge(turned[g], units(unit))
                copy(wt[:, GRP * g:GRP * g + n, :], tp[:, g % TB, 0:n * P]).then_inc(copied[g], 1)

        @block.sync
        def _(sp):
            sp.dma_start(gb[:, :], io["L1_gnn_graph_bias"].rearrange("a b c -> (a b) c").to_broadcast([P, 1])
                         ).then_inc(gb_in, 16)
            for b in range(2):
                sp.dma_start(adj[:, b, :], io["adj"][b * P:(b + 1) * P, :]).then_inc(adj_in[b], 16)

            def store(i, b):
                sp.wait_ge(n_ok[b], i + 1)
                sp.dma_start(keep["OD"][bass.ds((i * 2 + b) * P, P), :],
                             res[:, b, :, :].rearrange("p h o -> p (h o)")).then_inc(stored[b], 16)

            def load(i, b, row):
                sp.wait_ge(masked[1][NC - 1], i * 4 + (2 * b - 2))
                sp.dma_start(adj[:, b, :], io["adj"][bass.ds(row, P), :]).then_inc(adj_in[b], 16)
            with sp.Fori(0, NPAIR - 2) as i:
                for b in range(2):
                    load(i + 1, b, (i * 2 + b + 2) * P)
                    store(i, b)
            load(NPAIR - 1, 0, (NT - 2) * P)
            store(NPAIR - 2, 0)
            load(NPAIR - 1, 1, LAST)
            store(NPAIR - 2, 1)
            for b in range(2):
                store(NPAIR - 1, b)
            for b in range(2):
                sp.wait_ge(stored[b], NPAIR * 16)

        @block.gpsimd
        def _(pool):
            pool.wait_ge(gb_in, 16)

            def bias_tile(i, b):
                pool.wait_ge(adj_in[b], i * 16 + 16)
                if b:
                    pool.wait_ge(bias_done[0], i + 1)
                elif some(i):
                    pool.wait_ge(bias_done[1], i)
                pool.tensor_scalar(off[:, :], adj[:, b, :], 0.0, MASKED, ALU.is_equal,
                                   ALU.mult).then_inc(off_done[b], 1)
                pool.wait_ge(off_done[b], i + 1)
                pool.tensor_scalar(adj[:, b, :], adj[:, b, :], gb[:, :], None, ALU.mult).then_inc(scaled_adj[b], 1)
                pool.wait_ge(scaled_adj[b], i + 1)
                pool.tensor_tensor(adj[:, b, :], adj[:, b, :], off[:, :], ALU.add).then_inc(bias_done[b], 1)
            for t in range(NT):
                bias_tile(t // 2, t % 2)

        @block.scalar
        def _(act):
            def exp_part(unit):
                hb = unit[2] % 2
                act.wait_ge(neg_max[hb], parity(unit))
                act.activation(sc[:, hb, :], sc[:, hb, :], ACT.Exp, bias=mx[:, hb, NC:NC + 1]
                               ).then_inc(exp_done[hb], 1)

            def step(unit):
                copies(act, act.copy, unit, by_act)
                if later(unit, 1):
                    exp_part(later(unit, 1))
            exp_part((0, 0, 0))
            over_units(act, step)

        @block.vector
        def _(dve):
            def scores(unit):
                i, b, h = unit
                hb = h % 2
                if h == 0:
                    dve.wait_ge(bias_done[b], i + 1)
                for c, (c0, cn) in enumerate(CHUNKS):
                    s = (h * NC + c) % 2
                    dve.wait_ge(qk_done[s], i * (4 * NC) + (b * 2 * NC + (h * NC + c) // 2 + 1))
                    dve.nop(nofuse=True)
                    dve.tensor_tensor_reduce(sc[:, hb, c0:c0 + cn], qk[:, s, 0:cn], adj[:, b, c0:c0 + cn], 1.0,
                                             -BIG, ALU.add, ALU.max, mx[:, hb, c:c + 1]).then_inc(masked[hb][c], 1)
                for c in range(NC):
                    dve.wait_ge(masked[hb][c], parity(unit))
                dve.tensor_reduce(mx[:, hb, NC:NC + 1], mx[:, hb, 0:NC], AX.X, ALU.max,
                                  negate=True).then_inc(neg_max[hb], 1)

            def finish(i, b):
                sums = po[:, 0:H * VW].rearrange("p (h v) -> p h v", h=H)
                dve.wait_ge(heads_in, i * 2 + (b + 1))
                if some(i):
                    dve.wait_ge(stored[b], i * 16)
                dve.reciprocal(den[:, b, :], sums[:, :, HD]).then_inc(r_ok[b], 1)
                dve.wait_ge(r_ok[b], i + 1)
                dve.tensor_tensor(res[:, b, :, :], sums[:, :, 0:HD],
                                  den[:, b, :].rearrange("p (h a) -> p h a", a=1).to_broadcast([P, H, HD]),
                                  ALU.mult).then_inc(n_ok[b], 1)

            def step(unit):
                copies(dve, dve.tensor_copy, unit, by_dve)
                if unit[2] == 0 and later(unit, -H):
                    finish(*later(unit, -H)[:2])
                if later(unit, 2):
                    scores(later(unit, 2))
            scores((0, 0, 0))
            scores((0, 0, 1))
            over_units(dve, step)
            finish(NPAIR - 1, 1)

        @block.tensor
        def _(pe):
            def products(unit):
                i, b, h = unit
                for c, (c0, cn) in enumerate(CHUNKS):
                    s = (h * NC + c) % 2
                    maximum, number = chunk_read(i, b, h * NC + c - 2)
                    if some(number):
                        pe.wait_ge(maximum, number)
                    for n0 in range(c0, c0 + cn, 512):
                        nn = min(512, c0 + cn - n0)
                        out = qk[:, s, n0 - c0:n0 - c0 + nn]
                        query = QT[:, h, bass.ds((i * 2 + b) * P, P)]
                        pe.matmul(out, query, KH[:, h, n0:n0 + nn], start=True, stop=False)
                        mm = pe.matmul(out, query, KL[:, h, n0:n0 + nn], start=False, stop=True)
                    mm.then_inc(qk_done[s], 1)

            def chunk_read(i, b, k):
                if k >= 0:
                    h, c = divmod(k, NC)
                    return masked[h % 2][c], parity((i, b, h))
                h, c = divmod(k + H * NC, NC)
                return masked[h % 2][c], i * H + (b * (H // 2) - (H - 1 - h) // 2)

            def step(unit):
                i, b, h = unit
                pe.wait_ge(exp_done[h % 2], parity(unit))
                for g in range(NG):
                    if g >= TB:
                        pe.wait_ge(copied[g - TB], units(unit))
                    for j in range(GRP * g, min(GRP * g + GRP, NT)):
                        col = min(j * P, LAST)
                        mm = pe.transpose(tp[:, g % TB, (j % GRP) * P:(j % GRP + 1) * P],
                                          sc[:, h % 2, col:col + P], ident[:, :])
                    mm.then_inc(turned[g], 1)
                if later(unit, 2):
                    products(later(unit, 2))
                if h == 0 and later(unit, -H):
                    before = later(unit, -H)
                    pe.wait_ge(n_ok[before[1]], before[0] + 1)
                for g in range(NG):
                    pe.wait_ge(copied[g], units(unit))
                    for j in range(GRP * g, min(GRP * g + GRP, NT)):
                        mm = pe.matmul(po[:, h * VW:(h + 1) * VW], wt[:, j, :], V[:, j, h, :],
                                       start=(j == 0), stop=(j == NT - 1))
                if h == H - 1:
                    mm.then_inc(heads_in, 1)
            products((0, 0, 0))
            products((0, 0, 1))
            over_units(pe, step)


def moe_route(nc, io, keep, moe):
    X, ident, neg_half = (keep[n] for n in ("X", "ident", "neg_half"))
    XF, POSI, GW, GD, TE = (moe[n] for n in ("XF", "POSI", "GW", "GD", "TE"))
    NA = TOPK * NT
    with Phase(nc, "m0") as ph:
        gw = ph.sb("gw", [P, KD, E])
        gb = ph.sb("gb", [P, E])
        ones = ph.sb("ones", [P, P])
        before = ph.sb("before", [P, P])
        ie = ph.sb("ie", [P, E])
        steps = ph.sb("steps", [P, NT])
        tiles_i = ph.sb("tiles_i", [1, XTILES])
        st = ph.sb("st", [P, NT, 6])
        mom = ph.sb("mom", [P, 5, NT])
        rs = ph.sb("rs", [P, 4, NT])
        xn = ph.sb("xn", [P, 2, D])
        xt = ph.sb("xt", [P, 2, KD, P])
        lg = ph.sb("lg", [P, 2, NT, E])
        eq = ph.sb("eq", [P, NT, E])
        cand = ph.sb("cand", [P, NT, E])
        top = ph.sb("top", [P, 2, NT])
        idx = ph.sb("idx", [P, 2, NT])
        idxp = ph.sb("idxp", [P, 2, NT])
        pick = ph.sb("pick", [P, TOPK, NT, E])
        gap = ph.sb("gap", [P, 4, NT])
        tot = ph.sb("tot", [P, 3, NA, E])
        rank = ph.sb("rank", [P, NA, E])
        cnt = ph.sb("cnt", [P, E, NT])
        til = ph.sb("til", [P, 6, E])
        posf = ph.sb("posf", [P, NA])
        tef = ph.sb("tef", [1, 2, XTILES])
        pt = ph.ps("pt", [P, 2, 512])
        pg = ph.ps("pg", [P, 2, 512])
        pr = ph.ps("pr", [P, 2, 512])
        pc = ph.ps("pc", [P, 2, 512])
        (w_in, ones_ok, consts, stats, moments, inv, pchain, folded, chain, exp_in, exp_ok, picked, ranks,
         scattered, pos_ok, xf_done) = ph.sems(
            "w_in ones_ok consts stats moments inv pchain folded chain exp_in exp_ok picked ranks "
            "scattered pos_ok xf_done")
        xn_done, turned, xt_done, g_mm, lg_done = (
            ph.sems(f"{n}0 {n}1") for n in "xn_done turned xt_done g_mm lg_done".split())
        block = ph.block()

        @block.sync
        def _(sp):
            sp.dma_start(gw[:, :, :], io["L0_ffn_gate_w"].rearrange("(k p) e -> p k e", p=P)).then_inc(w_in, 16)
            sp.dma_start(gb[:, :], bcast_rows(io["L0_ffn_gate_b"], P)).then_inc(w_in, 16)
            for e in range(E):
                sp.dma_start(moe["W1"][:, e, :, :], io["L0_ffn_w1"][e, :, :].rearrange("(k p) f -> p k f", p=P)
                             ).then_inc(moe["w_in"], 16)
                sp.dma_start(moe["W2"][:, e, :, :], io["L0_ffn_w2"][e, :, :].rearrange("(k p) f -> p k f", p=P)
                             ).then_inc(moe["w_in"], 16)

        @block.gpsimd
        def _(pool):
            pool.memset(ones[:, :], 1.0).then_inc(ones_ok, 1)
            pool.memset(before[:, :], 1.0).then_inc(ones_ok, 1)
            pool.wait_ge(ones_ok, 2)
            pool.affine_select(out=before[:, :], in_=before[:, :], compare_op=ALU.is_gt, fill=0.0, base=0,
                               pattern=[[1, P]], channel_multiplier=-1).then_inc(consts, 1)
            for tile, n, step in ((ie, E, 1), (steps, NT, P), (tiles_i, XTILES, 1)):
                pool.iota(tile[:, :], [[step, n]], base=0, channel_multiplier=0,
                          allow_small_or_imprecise_dtypes=True).then_inc(consts, 1)
            pool.wait_ge(moments, 1)
            inverse_deviation(pool, mom, rs, neg_half, 0, NT, pchain, 0).then_inc(inv, 1)
            pool.wait_ge(inv, 1)
            for i in range(NPAIR):
                for b in range(2):
                    if some(i):
                        pool.wait_ge(turned[b], i)
                    t = i * 2 + b
                    xs = X[:, bass.ds(t, 1), :]
                    standard_rows(pool, xn[:, b:b + 1, :], xs, rs, t).then_inc(xn_done[b], 1)
                    standard_rows(pool, XF[:, bass.ds(t, 1), :], xs, rs, t).then_inc(xf_done, 1)
            pool.wait_ge(xf_done, NT)
            pool.wait_ge(pos_ok, 1)
            for j in range(NA):
                pool.indirect_dma_start(keep["XD"], bass.IndirectOffsetOnAxis(POSI[:, j:j + 1], 0),
                                        XF[:, j % NT, :], None).then_inc(scattered, 16)
            pool.wait_ge(scattered, 16 * NA)

        @block.tensor
        def _(pe):
            pe.wait_ge(w_in, 32)

            def turn(i, b):
                pe.wait_ge(xn_done[b], i + 1)
                if some(i):
                    pe.wait_ge(xt_done[b], i)
                for k in range(KD):
                    mm = pe.transpose(pt[:, b, k * P:(k + 1) * P], xn[:, b, k * P:(k + 1) * P], ident[:, :])
                mm.then_inc(turned[b], 1)

            def product(i, b):
                pe.wait_ge(xt_done[b], i + 1)
                if some(i):
                    pe.wait_ge(lg_done[b], i)
                for k in range(KD):
                    mm = pe.matmul(pg[:, b, 0:E], xt[:, b, k, :], gw[:, k, :], start=(k == 0), stop=(k == KD - 1))
                mm.then_inc(g_mm[b], 1)
            turn(0, 0)
            def pair(i):
                turn(i, 1)
                product(i, 0)
                turn(i + 1, 0)
                product(i, 1)
            pair(0)
            with pe.Fori(1, NPAIR - 1) as i:
                pair(i)
            turn(NPAIR - 1, 1)
            product(NPAIR - 1, 0)
            product(NPAIR - 1, 1)
            pe.wait_ge(consts, 1)
            pe.wait_ge(ones_ok, 1)
            pe.wait_ge(picked, 2)
            for k in range(TOPK):
                pe.matmul(pr[:, k, 0:NT * E], before[:, :], pick[:, k, :, :].rearrange("p t e -> p (t e)"),
                          start=True, stop=True)
                mm = pe.matmul(pc[:, k, 0:NT * E], ones[:, :], pick[:, k, :, :].rearrange("p t e -> p (t e)"),
                               start=True, stop=True)
            mm.then_inc(ranks, 1)

        @block.scalar
        def _(act):
            with act.Fori(0, NPAIR) as i:
                for b in range(2):
                    act.wait_ge(turned[b], i + 1)
                    act.copy(xt[:, b, :, :], pt[:, b, 0:D]).then_inc(xt_done[b], 1)
            act.wait_ge(exp_in, 1)
            act.activation(gap[:, 1, :], gap[:, 0, :], ACT.Exp).then_inc(exp_ok, 1)

        @block.vector
        def _(dve):
            slot_moments(dve, X, st, mom, stats, folded, moments)
            dve.wait_ge(w_in, 32)
            with dve.Fori(0, NPAIR) as i:
                for b in range(2):
                    dve.wait_ge(g_mm[b], i + 1)
                    dve.tensor_tensor(lg[:, 0, bass.ds(i * 2 + b, 1), :], pg[:, b:b + 1, 0:E],
                                      gb[:, :].rearrange("p (a e) -> p a e", a=1), ALU.add).then_inc(lg_done[b], 1)
            for b in range(2):
                dve.wait_ge(lg_done[b], NPAIR)
            dve.wait_ge(consts, 4)
            n = [0]

            def link(ins):
                n[0] += 1
                ins.then_inc(chain, 1)
                dve.wait_ge(chain, n[0])

            def over_experts(ap):
                return ap.rearrange("p (t a) -> p t a", a=1).to_broadcast([P, NT, E])
            ie_all = ie[:, :].rearrange("p (a e) -> p a e", a=1).to_broadcast([P, NT, E])
            for k in range(TOPK):
                link(dve.tensor_reduce(top[:, k, :], lg[:, k, :, :], AX.X, ALU.max))
                link(dve.tensor_tensor(eq[:, :, :], lg[:, k, :, :], over_experts(top[:, k, :]), ALU.is_equal))
                link(dve.scalar_tensor_tensor(cand[:, :, :], eq[:, :, :], -float(E), ie_all, ALU.mult, ALU.add))
                link(dve.tensor_reduce(idx[:, k, :], cand[:, :, :], AX.X, ALU.min))
                link(dve.tensor_scalar(idxp[:, k, :], idx[:, k, :], float(E), None, ALU.add))
                dve.tensor_tensor(pick[:, k, :, :], over_experts(idxp[:, k, :]), ie_all,
                                  ALU.is_equal).then_inc(picked, 1)
                dve.wait_ge(picked, k + 1)
                if k == 0:
                    link(dve.scalar_tensor_tensor(lg[:, 1, :, :], pick[:, 0, :, :], -BIG, lg[:, 0, :, :],
                                                  ALU.mult, ALU.add))
            dve.tensor_tensor(gap[:, 0, :], top[:, 1, :], top[:, 0, :], ALU.subtract).then_inc(exp_in, 1)
            dve.wait_ge(exp_ok, 1)
            link(dve.tensor_scalar(gap[:, 2, :], gap[:, 1, :], 1.0, None, ALU.add))
            link(dve.reciprocal(GW[:, 0, :], gap[:, 2, :]))
            link(dve.tensor_tensor(GW[:, 1, :], gap[:, 1, :], GW[:, 0, :], ALU.mult))
            for k in range(TOPK):
                share = (eq, cand)[k]
                link(dve.tensor_tensor(share[:, :, :], pick[:, k, :, :], over_experts(GW[:, k, :]), ALU.mult))
            link(dve.tensor_tensor(GD[:, :, :], eq[:, :, :], cand[:, :, :], ALU.add))

            dve.wait_ge(ranks, 1)
            for k in range(TOPK):
                cols = slice(k * NT, (k + 1) * NT)
                dve.tensor_copy(rank[:, cols, :], pr[:, k, 0:NT * E])
                dve.tensor_copy(tot[:, 0, cols, :], pc[:, k, 0:NT * E])
                link(dve.tensor_copy(tot[:, 1, cols, :], pc[:, k, 0:NT * E]))
            src, s = 1, 1
            while s < NA:
                dst = 3 - src
                dve.tensor_copy(tot[:, dst, 0:s, :], tot[:, src, 0:s, :])
                link(dve.tensor_tensor(tot[:, dst, s:NA, :], tot[:, src, s:NA, :], tot[:, src, 0:NA - s, :], ALU.add))
                src, s = dst, 2 * s
            count = tot[:, src, NA - 1, :]
            link(dve.tensor_tensor(cnt[:, :, :], count.rearrange("p (e a) -> p e a", a=1).to_broadcast([P, E, NT]),
                                   steps[:, :].rearrange("p (a t) -> p a t", a=1).to_broadcast([P, E, NT]),
                                   ALU.is_gt))
            dve.tensor_reduce(til[:, 0, :], cnt[:, :, :], AX.X, ALU.add)
            link(dve.tensor_reduce(til[:, 1, :], cnt[:, :, :], AX.X, ALU.add))
            tsrc, s = 1, 1
            while s < E:
                dst = 3 - tsrc
                dve.tensor_copy(til[:, dst, 0:s], til[:, tsrc, 0:s])
                link(dve.tensor_tensor(til[:, dst, s:E], til[:, tsrc, s:E], til[:, tsrc, 0:E - s], ALU.add))
                tsrc, s = dst, 2 * s
            ends = til[:, tsrc, :]
            link(dve.tensor_tensor(til[:, 3, :], ends, til[:, 0, :], ALU.subtract))
            link(dve.tensor_scalar(til[:, 4, :], til[:, 3, :], float(P), None, ALU.mult))
            here = tot[:, 3 - src, :, :]
            link(dve.tensor_tensor(here, tot[:, src, :, :], tot[:, 0, :, :], ALU.subtract))
            link(dve.tensor_tensor(rank[:, :, :], here, rank[:, :, :], ALU.add))
            link(dve.tensor_tensor(rank[:, :, :], rank[:, :, :],
                                   til[:, 4, :].rearrange("p (a e) -> p a e", a=1).to_broadcast([P, NA, E]), ALU.add))
            link(dve.tensor_tensor(rank[:, :, :], rank[:, :, :], pick[:, :, :, :].rearrange("p k t e -> p (k t) e"),
                                   ALU.mult))
            link(dve.tensor_reduce(posf[:, :], rank[:, :, :], AX.X, ALU.add))
            dve.tensor_copy(POSI[:, :], posf[:, :]).then_inc(pos_ok, 1)
            tcmp = tot[0:1, :, :, :].rearrange("p j a e -> p (j a) e")[:, 0:XTILES, :]
            link(dve.tensor_tensor(tcmp, ends[0:1, :].rearrange("p (a e) -> p a e", a=1).to_broadcast([1, XTILES, E]),
                                   tiles_i[:, :].rearrange("p (t a) -> p t a", a=1).to_broadcast([1, XTILES, E]),
                                   ALU.is_le))
            link(dve.tensor_reduce(tef[:, 0, :], tcmp, AX.X, ALU.add))
            link(dve.tensor_scalar(tef[:, 1, :], tef[:, 0, :], float(E - 1), None, ALU.min))
            link(dve.tensor_copy(TE[:, :], tef[:, 1, :]))


def moe_experts(nc, io, keep, moe):
    ident, TE, W1, W2, w_in = keep["ident"], moe["TE"], moe["W1"], moe["W2"], moe["w_in"]
    PAIRS = XTILES // 2
    with Phase(nc, "m1") as ph:
        w1 = ph.sb("w1", [P, 2, KD, F])
        b1 = ph.sb("b1", [P, E * FB])
        b1n = ph.sb("b1n", [E * FB, P])
        rows = ph.sb("rows", [P, 2, D])
        xt = ph.sb("xt", [P, 2, KD, P])
        hid = ph.sb("hid", [P, 2, FB, P])
        y = ph.sb("y", [P, 2, D])
        pt = ph.ps("pt", [P, 2, 512])
        p1 = ph.ps("p1", [P, 2, 512])
        p2 = ph.ps("p2", [P, 2, 512])
        pb = ph.ps("pb", [P, 512])
        b_in, b_ps, b_ok = ph.sems("b_in b_ps b_ok")
        staged, rows_in, turned, xt_done, hid_mm, hid_done, y_mm, y_done, stored = (
            ph.sems(f"{n}0 {n}1") for n in
            "staged rows_in turned xt_done hid_mm hid_done y_mm y_done stored".split())
        block = ph.block()

        def expert_of(eng, i, b):
            return eng.value_load(TE[0:1, bass.ds(i * 2 + b, 1)], min_val=0, max_val=E - 1)

        @block.sync
        def _(sp):
            sp.dma_start(b1n[:, :], io["L0_ffn_b1"].rearrange("e (f p) -> (e f) p", p=P)).then_inc(b_in, 16)

            def load(i, b):
                if some(i):
                    sp.wait_ge(turned[b], i)
                sp.dma_start(rows[:, b, :], keep["XD"][bass.ds((i * 2 + b) * P, P), :]).then_inc(rows_in[b], 16)
            for b in range(2):
                load(0, b)
            with sp.Fori(1, PAIRS) as i:
                for b in range(2):
                    load(i, b)

        @block.tensor
        def _(pe):
            pe.wait_ge(b_in, 16)
            pe.transpose(pb[:, 0:E * FB], b1n[:, :], ident[0:E * FB, 0:E * FB]).then_inc(b_ps, 1)

            def turn(i, b):
                pe.wait_ge(rows_in[b], i * 16 + 16)
                if some(i):
                    pe.wait_ge(xt_done[b], i)
                for k in range(KD):
                    mm = pe.transpose(pt[:, b, k * P:(k + 1) * P], rows[:, b, k * P:(k + 1) * P], ident[:, :])
                mm.then_inc(turned[b], 1)

            def up(i, b):
                pe.wait_ge(staged[b], i + 1)
                pe.wait_ge(xt_done[b], i + 1)
                if some(i):
                    pe.wait_ge(hid_done[b], i * FB)
                for f in range(FB):
                    for k in range(KD):
                        mm = pe.matmul(p1[:, b, f * P:(f + 1) * P], w1[:, b, k, f * P:(f + 1) * P], xt[:, b, k, :],
                                       start=(k == 0), stop=(k == KD - 1))
                mm.then_inc(hid_mm[b], 1)

            def down(i, b):
                e = expert_of(pe, i, b)
                pe.wait_ge(hid_done[b], i * FB + FB)
                if some(i):
                    pe.wait_ge(y_done[b], i)
                for f in range(FB):
                    mm = pe.matmul(p2[:, b, 0:D], hid[:, b, f, :], W2[:, bass.ds(e, 1), f, :],
                                   start=(f == 0), stop=(f == FB - 1))
                mm.then_inc(y_mm[b], 1)

            turn(0, 0)
            turn(0, 1)
            up(0, 0)

            def pair(i):
                up(i, 1)
                turn(i + 1, 0)
                down(i, 0)
                up(i + 1, 0)
                turn(i + 1, 1)
                down(i, 1)
            pair(0)
            with pe.Fori(1, PAIRS - 1) as i:
                pair(i)
            up(PAIRS - 1, 1)
            down(PAIRS - 1, 0)
            down(PAIRS - 1, 1)

        @block.vector
        def _(dve):
            dve.wait_ge(w_in, 2 * 16 * E)

            def stage(i, b):
                e = expert_of(dve, i, b)
                if some(i):
                    dve.wait_ge(hid_mm[b], i)
                dve.tensor_copy(w1[:, b:b + 1, :, :], W1[:, bass.ds(e, 1), :, :]).then_inc(staged[b], 1)
                dve.wait_ge(turned[b], i + 1)
                dve.tensor_copy(xt[:, b, :, :], pt[:, b, 0:D]).then_inc(xt_done[b], 1)

            def y_out(i, b):
                dve.wait_ge(y_mm[b], i + 1)
                if some(i):
                    dve.wait_ge(stored[b], i * 16)
                dve.tensor_copy(y[:, b, :], p2[:, b, 0:D]).then_inc(y_done[b], 1)
            stage(0, 0)
            stage(0, 1)

            def pair(i):
                stage(i + 1, 0)
                y_out(i, 0)
                stage(i + 1, 1)
                y_out(i, 1)
            pair(0)
            with dve.Fori(1, PAIRS - 1) as i:
                pair(i)
            y_out(PAIRS - 1, 0)
            y_out(PAIRS - 1, 1)

        @block.scalar
        def _(act):
            act.wait_ge(b_ps, 1)
            act.copy(b1[:, :], pb[:, 0:E * FB]).then_inc(b_ok, 1)
            act.wait_ge(b_ok, 1)
            with act.Fori(0, PAIRS) as i:
                for b in range(2):
                    e = expert_of(act, i, b)
                    act.wait_ge(hid_mm[b], i + 1)
                    for f in range(FB):
                        act.activation(hid[:, b, f, :], p1[:, b, f * P:(f + 1) * P], ACT.Relu,
                                       bias=b1[:, bass.ds(e * FB + f, 1)]).then_inc(hid_done[b], 1)

        @block.gpsimd
        def _(pool):
            with pool.Fori(0, PAIRS) as i:
                for b in range(2):
                    pool.wait_ge(y_done[b], i + 1)
                    pool.dma_start(keep["YD"][bass.ds((i * 2 + b) * P, P), :], y[:, b, :]).then_inc(stored[b], 16)
            for b in range(2):
                pool.wait_ge(stored[b], PAIRS * 16)


def moe_combine(nc, io, keep, moe):
    X, ident, neg_half = (keep[n] for n in ("X", "ident", "neg_half"))
    XF, POSI, GW, GD = (moe[n] for n in ("XF", "POSI", "GW", "GD"))
    NA = TOPK * NT
    with Phase(nc, "m2") as ph:
        b2 = ph.sb("b2", [E, D])
        affine = ph.sb("affine", [P, 2, D])
        got = ph.sb("got", [P, NA, D])
        st = ph.sb("st", [P, NT, 6])
        mom = ph.sb("mom", [P, 5, NT])
        rs = ph.sb("rs", [P, 4, NT])
        z = ph.sb("z", [P, 2, D])
        zz = ph.sb("zz", [P, 2, D])
        gt = ph.sb("gt", [E, 2, P])
        pb = ph.ps("pb", [P, 2, 512])
        pt = ph.ps("pt", [P, 2, 512])
        w_in, gathered, stats, folded, moments, pchain, inv, first, second = ph.sems(
            "w_in gathered stats folded moments pchain inv first second")
        gt_ps, gt_sb, b_mm, third, z_done, zz_done, biased, x_out = (
            ph.sems(f"{n}0 {n}1") for n in "gt_ps gt_sb b_mm third z_done zz_done biased x_out".split())
        block = ph.block()

        @block.sync
        def _(sp):
            sp.dma_start(b2[:, :], io["L0_ffn_b2"]).then_inc(w_in, 16)
            for j, name in enumerate(("L0_ffn_gamma", "L0_ffn_beta")):
                sp.dma_start(affine[:, j, :], bcast_rows(io[name], P)).then_inc(w_in, 16)

        @block.gpsimd
        def _(pool):
            for j in range(NA):
                pool.indirect_dma_start(got[:, j, :], None, keep["YD"],
                                        bass.IndirectOffsetOnAxis(POSI[:, j:j + 1], 0)).then_inc(gathered, 16)
            pool.wait_ge(w_in, 48)
            with pool.Fori(0, NT) as t:
                xs = X[:, bass.ds(t, 1), :]
                pool.tensor_tensor(xs, xs, affine[:, 1:2, :], ALU.add).then_inc(biased[0], 1)
            pool.wait_ge(moments, 1)
            inverse_deviation(pool, mom, rs, neg_half, 0, NT, pchain, 0).then_inc(inv, 1)
            pool.wait_ge(inv, 1)
            for i in range(NPAIR):
                for b in range(2):
                    if some(i):
                        pool.wait_ge(zz_done[b], i)
                    t = i * 2 + b
                    standard_rows(pool, z[:, b:b + 1, :], XF[:, bass.ds(t, 1), :], rs, t).then_inc(z_done[b], 1)

        @block.tensor
        def _(pe):
            pe.wait_ge(w_in, 48)
            for t in range(NT):
                i, b = divmod(t, 2)
                if some(i):
                    pe.wait_ge(gt_sb[b], i)
                pe.transpose(pt[0:E, b, 0:P], GD[:, t, :], ident[:, :]).then_inc(gt_ps[b], 1)
                pe.wait_ge(gt_sb[b], i + 1)
                if some(i):
                    pe.wait_ge(third[b], i)
                pe.matmul(pb[:, b, 0:D], gt[:, b, :], b2[:, :], start=True, stop=True).then_inc(b_mm[b], 1)

        @block.scalar
        def _(act):
            for t in range(NT):
                i, b = divmod(t, 2)
                act.wait_ge(gt_ps[b], i + 1)
                if some(i):
                    act.wait_ge(b_mm[b], i)
                act.copy(gt[:, b, :], pt[0:E, b, 0:P]).then_inc(gt_sb[b], 1)

        @block.vector
        def _(dve):
            dve.wait_ge(gathered, 16 * NA)
            with dve.Fori(0, NPAIR) as i:
                for b in range(2):
                    t = i * 2 + b
                    xs = XF[:, bass.ds(t, 1), :]
                    dve.scalar_tensor_tensor(xs, got[:, bass.ds(t, 1), :], GW[:, 0, bass.ds(t, 1)], xs, ALU.mult,
                                             ALU.add).then_inc(first, 1)
                    dve.wait_ge(first, t + 1)
                    dve.scalar_tensor_tensor(xs, got[:, bass.ds(t + NT, 1), :], GW[:, 1, bass.ds(t, 1)], xs,
                                             ALU.mult, ALU.add).then_inc(second, 1)
                    dve.wait_ge(second, t + 1)
                    dve.wait_ge(b_mm[b], i + 1)
                    dve.tensor_tensor(xs, pb[:, b:b + 1, 0:D], xs, ALU.add).then_inc(third[b], 1)
                    dve.wait_ge(third[b], i + 1)
                    dve.bn_stats(st[:, bass.ds(t, 1), :], xs).then_inc(stats, 1)
            dve.wait_ge(stats, NT)
            row_moments(dve, st, mom, 0, NT, folded, 0).then_inc(moments, 1)
            dve.wait_ge(w_in, 48)
            dve.wait_ge(biased[0], NT)
            def pair(i):
                for b in range(2):
                    t = i * 2 + b
                    dve.wait_ge(z_done[b], i + 1)
                    if some(i):
                        dve.wait_ge(x_out[b], i)
                    dve.tensor_tensor(zz[:, b:b + 1, :], z[:, b:b + 1, :], affine[:, 0:1, :], ALU.mult
                                      ).then_inc(zz_done[b], 1)
                    dve.wait_ge(zz_done[b], i + 1)
                    xs = X[:, bass.ds(t, 1), :]
                    dve.tensor_tensor(xs, xs, zz[:, b:b + 1, :], ALU.add).then_inc(x_out[b], 1)
            pair(0)
            with dve.Fori(1, NPAIR) as i:
                pair(i)


def layer1_project(nc, io, keep):
    X, ident = keep["X"], keep["ident"]
    with Phase(nc, "o1") as ph:
        wout = ph.sb("wout", [P, KD, D])
        bout = ph.sb("bout", [P, D])
        o = ph.sb("o", [P, NT, D])
        od = ph.sb("od", [P, 2, D])
        ot = ph.sb("ot", [P, 2, KD, P])
        pt = ph.ps("pt", [P, 2, 512])
        py = ph.ps("py", [P, 2, 512])
        w_in, o_in = ph.sems("w_in o_in")
        staged, turned, ot_done, y_mm, biased, x_out = (
            ph.sems(f"{n}0 {n}1") for n in "staged turned ot_done y_mm biased x_out".split())
        block = ph.block()

        @block.sync
        def _(sp):
            sp.dma_start(o[:, :, :], keep["OD"].rearrange("(t p) d -> p t d", p=P)).then_inc(o_in, 16)
            sp.dma_start(wout[:, :, :], io["L1_gnn_Wout"].rearrange("(k p) o -> p k o", p=P)).then_inc(w_in, 16)
            sp.dma_start(bout[:, :], bcast_rows(io["L1_gnn_bout"], P)).then_inc(w_in, 16)

        @block.gpsimd
        def _(pool):
            pool.wait_ge(w_in, 32)
            pool.wait_ge(o_in, 16)
            for i in range(NPAIR):
                for b in range(2):
                    xs = X[:, bass.ds(i * 2 + b, 1), :]
                    pool.tensor_tensor(xs, xs, bout[:, :].rearrange("p (a d) -> p a d", a=1),
                                       ALU.add).then_inc(biased[b], 1)
                    if some(i):
                        pool.wait_ge(turned[b], i)
                    pool.tensor_copy(od[:, b:b + 1, :], o[:, bass.ds(i * 2 + b, 1), :]).then_inc(staged[b], 1)

        @block.scalar
        def _(act):
            with act.Fori(0, NPAIR) as i:
                for b in range(2):
                    act.wait_ge(turned[b], i + 1)
                    act.copy(ot[:, b, :, :], pt[:, b, 0:D]).then_inc(ot_done[b], 1)

        @block.vector
        def _(dve):
            with dve.Fori(0, NPAIR) as i:
                for b in range(2):
                    dve.wait_ge(y_mm[b], i + 1)
                    dve.wait_ge(biased[b], i + 1)
                    xs = X[:, bass.ds(i * 2 + b, 1), :]
                    dve.tensor_tensor(xs, py[:, b:b + 1, 0:D], xs, ALU.add).then_inc(x_out[b], 1)

        @block.tensor
        def _(pe):
            pe.wait_ge(w_in, 32)

            def turn(i, b):
                pe.wait_ge(staged[b], i + 1)
                if some(i):
                    pe.wait_ge(ot_done[b], i)
                for k in range(KD):
                    mm = pe.transpose(pt[:, b, k * P:(k + 1) * P], od[:, b, k * P:(k + 1) * P], ident[:, :])
                mm.then_inc(turned[b], 1)

            def product(i, b):
                pe.wait_ge(ot_done[b], i + 1)
                if some(i):
                    pe.wait_ge(x_out[b], i)
                for k in range(KD):
                    mm = pe.matmul(py[:, b, 0:D], ot[:, b, k, :], wout[:, k, :],
                                   start=(k == 0), stop=(k == KD - 1))
                mm.then_inc(y_mm[b], 1)
            turn(0, 0)
            def pair(i):
                turn(i, 1)
                product(i, 0)
                turn(i + 1, 0)
                product(i, 1)
            pair(0)
            with pe.Fori(1, NPAIR - 1) as i:
                pair(i)
            turn(NPAIR - 1, 1)
            product(NPAIR - 1, 0)
            product(NPAIR - 1, 1)


BATCHES = [(0, 4), (4, 8), (8, NPAIR)]
RING = 4


def layer1_ffn(nc, io, keep):
    X, ident, neg_half = (keep[n] for n in ("X", "ident", "neg_half"))
    with Phase(nc, "f1") as ph:
        wn = ph.sb("wn", [P, KD, D])
        wt = ph.sb("wt", [P, KD, KD, P])
        wl = ph.sb("wl", [P, KD, KD * P])
        lnwb = ph.sb("lnwb", [P, 2, KD])
        lb3 = ph.sb("lb3", [P, KD, 3])
        ones = ph.sb("ones", [P, P])
        b3 = ph.sb("b3", [3, D])
        c3 = ph.sb("c3", [3, 3, D])
        parts = ph.sb("parts", [3, 3, D], BF16)
        sel = ph.sb("sel", [3, 3, D])
        crow = ph.sb("crow", [3, D], BF16)
        ones3 = ph.sb("ones3", [3, P], BF16)
        th = ph.sb("th", [P, NPAIR, 2, D])
        gg = ph.sb("gg", [P, NPAIR, 2, D])
        yt = ph.sb("yt", [P, RING, 2, KD, P])
        st = ph.sb("st", [P, NT, 6])
        mom = ph.sb("mom", [P, 5, NT])
        rs = ph.sb("rs", [P, 4, NT])
        pt = ph.ps("pt", [P, RING, 512])
        pm = ph.ps("pm", [P, RING, 512])
        (w_in, w_ps, w_sb, w_scaled, ones_done, c_mm, cchain, c_done, x_stats, x_folded, x_moments, x_pchain,
         x_inv, h_done, out_done, stored) = ph.sems(
            "w_in w_ps w_sb w_scaled ones_done c_mm cchain c_done x_stats x_folded x_moments x_pchain "
            "x_inv h_done out_done stored")
        each = lambda n: ph.sems(" ".join(f"{n}{g}" for g in range(NPAIR)))
        turned, yt_done, h_mm, tanh_done, g_done, silu_done, stat_done, y_done, res_done = (
            each(n) for n in "turned yt_done h_mm tanh_done g_done silu_done stat_done y_done res_done".split())
        folded, moments, pchain, inv = (ph.sems(" ".join(f"{n}{k}" for k in range(len(BATCHES))))
                                        for n in "folded moments pchain inv".split())
        block = ph.block()

        def last_user(g):
            same = [q for q in range(NPAIR) if q % RING == g % RING]
            at = same.index(g)
            return (same[at - 1], at > 0)

        def batch_of(g):
            return next(k for k, (a, z) in enumerate(BATCHES) if a <= g < z)

        @block.sync
        def _(sp):
            sp.dma_start(wn[:, :, :], io["L1_ffn_W"].rearrange("(k p) o -> p k o", p=P)).then_inc(w_in, 16)
            sp.dma_start(b3[:, :], bcast_rows(io["L1_ffn_b"], 3)).then_inc(w_in, 16)
            with nc.allow_non_contiguous_dma(reason="two columns of 128"):
                for j, name in enumerate(("L1_ffn_ln_w", "L1_ffn_ln_b")):
                    sp.dma_start(lnwb[:, j, :], io[name].rearrange("(k p) -> p k", p=P)).then_inc(w_in, 16)
            for g in range(NPAIR):
                sp.wait_ge(out_done, g + 1)
                for r in range(2):
                    t = 2 * g + r
                    if t < NT - 1:
                        sp.dma_start(io["out"][t * P:(t + 1) * P, :], X[:, t, :]).then_inc(stored, 16)
                    else:
                        sp.dma_start(io["out"][t * P:N, :], X[OVER:P, t, :]).then_inc(stored, 16)
            sp.wait_ge(stored, NT * 16)

        def elementwise_dve(dve, i, src):
            def blend(g):
                dve.wait_ge(tanh_done[g], i + 1)
                dve.scalar_tensor_tensor(gg[:, g, :, :], th[:, g, :, :], 0.01, src(g), ALU.mult,
                                         ALU.add).then_inc(g_done[g], 1)

            def stats(g):
                dve.wait_ge(silu_done[g], i + 1)
                for r in range(2):
                    dve.bn_stats(st[:, 2 * g + r, :], th[:, g, r, :]).then_inc(stat_done[g], 1)
                k = batch_of(g)
                if g == BATCHES[k][1] - 1:
                    a, z = BATCHES[k]
                    for q in range(a, z):
                        dve.wait_ge(stat_done[q], i * 2 + 2)
                    row_moments(dve, st, mom, 2 * a, 2 * z, folded[k], i * 3).then_inc(moments[k], 1)
            for g in range(NPAIR):
                blend(g)
                if g >= 2:
                    stats(g - 2)
            stats(NPAIR - 2)
            stats(NPAIR - 1)

        def elementwise_pool(pool, i):
            for k, (a, z) in enumerate(BATCHES):
                pool.wait_ge(moments[k], i + 1)
                pool.nop(nofuse=True)
                inverse_deviation(pool, mom, rs, neg_half, 2 * a, 2 * z, pchain[k], i * 3).then_inc(inv[k], 1)
                pool.wait_ge(inv[k], i + 1)
                pool.nop(nofuse=True)
                for g in range(a, z):
                    for r in range(2):
                        standard_rows(pool, gg[:, g, r:r + 1, :], th[:, g, r:r + 1, :], rs,
                                      2 * g + r).then_inc(y_done[g], 1)

        @block.gpsimd
        def _(pool):
            pool.memset(ones[:, :], 1.0).then_inc(ones_done, 1)
            pool.memset(ones3[:, :], 1.0).then_inc(ones_done, 1)
            pool.wait_ge(x_moments, 1)
            inverse_deviation(pool, mom, rs, neg_half, 0, NT, x_pchain, 0).then_inc(x_inv, 1)
            pool.wait_ge(x_inv, 1)
            for g in range(NPAIR):
                for r in range(2):
                    standard_rows(pool, gg[:, g, r:r + 1, :], X[:, 2 * g + r:2 * g + r + 1, :], rs,
                                  2 * g + r).then_inc(h_done, 1)
            elementwise_pool(pool, 0)
            with pool.Fori(1, ITERS) as i:
                elementwise_pool(pool, i)

        @block.vector
        def _(dve):
            slot_moments(dve, X, st, mom, x_stats, x_folded, x_moments)
            dve.wait_ge(w_in, 64)
            dve.wait_ge(ones_done, 2)
            for k in range(KD):
                dve.tensor_scalar(lb3[:, k, :], ones[:, 0:3], lnwb[:, 1, k:k + 1], None, ALU.mult).then_inc(w_scaled, 1)
            dve.wait_ge(w_sb, 1)
            for k in range(KD):
                dve.tensor_scalar(wl[:, k, :], wt[:, k, :, :].rearrange("p j o -> p (j o)"),
                                  lnwb[:, 0, k:k + 1], None, ALU.mult).then_inc(w_scaled, 1)
            dve.wait_ge(c_mm, 1)
            dve.tensor_tensor(c3[:, 0, :], pm[0:3, 0, 0:D], b3[:, :], ALU.add).then_inc(cchain, 1)
            n = 1
            for r in range(3):
                dve.wait_ge(cchain, n)
                dve.tensor_copy(parts[:, r, :], c3[:, r, :]).then_inc(cchain, 1)
                n += 1
                dve.wait_ge(cchain, n)
                if r < 2:
                    dve.tensor_tensor(c3[:, r + 1, :], c3[:, r, :], parts[:, r, :], ALU.subtract).then_inc(cchain, 1)
                    n += 1
            dve.tensor_scalar(sel[:, 0, :], parts[:, 0, :], ident[0:3, 0:1], None, ALU.mult).then_inc(cchain, 1)
            dve.wait_ge(cchain, n + 1)
            dve.scalar_tensor_tensor(sel[:, 1, :], parts[:, 1, :], ident[0:3, 1:2], sel[:, 0, :], ALU.mult,
                                     ALU.add).then_inc(cchain, 1)
            dve.wait_ge(cchain, n + 2)
            dve.scalar_tensor_tensor(crow[:, :], parts[:, 2, :], ident[0:3, 2:3], sel[:, 1, :], ALU.mult,
                                     ALU.add).then_inc(c_done, 1)

            elementwise_dve(dve, 0, lambda g: gg[:, g, :, :])
            with dve.Fori(1, ITERS) as i:
                elementwise_dve(dve, i, lambda g: pm[:, g % RING, :].rearrange("p (r d) -> p r d", r=2))
            for g in range(NPAIR):
                dve.wait_ge(h_mm[g], ITERS)
                dve.tensor_tensor(X[:, 2 * g:2 * g + 2, :], pm[:, g % RING, :].rearrange("p (r d) -> p r d", r=2),
                                  X[:, 2 * g:2 * g + 2, :], ALU.add).then_inc(out_done, 1)

        def act_stream(act, i, first):
            def turned_out(g):
                act.wait_ge(turned[g], i)
                act.copy(yt[:, g % RING, :, :, :], pt[:, g % RING, :]).then_inc(yt_done[g], 1)

            def tanh(g):
                if first:
                    act.wait_ge(h_done, 2 * g + 2)
                    src = gg[:, g, :, :]
                else:
                    act.wait_ge(h_mm[g], i)
                    act.wait_ge(y_done[g], i * 2)
                    src = pm[:, g % RING, :]
                act.activation(th[:, g, :, :], src, ACT.Tanh).then_inc(tanh_done[g], 1)

            def silu(g):
                act.wait_ge(g_done[g], i + 1)
                act.activation(th[:, g, :, :], gg[:, g, :, :], ACT.Silu).then_inc(silu_done[g], 1)
            for g in range(NPAIR + 2):
                if g < NPAIR and not first:
                    turned_out(g)
                if 1 <= g <= NPAIR:
                    tanh(g - 1)
                if g >= 2:
                    silu(g - 2)

        @block.scalar
        def _(act):
            act.wait_ge(w_ps, 1)
            act.copy(wt[:, :, :, :], pt[:, 0, :]).then_inc(w_sb, 1)
            act_stream(act, 0, True)
            with act.Fori(1, ITERS) as i:
                act_stream(act, i, False)
            for g in range(NPAIR):
                act.wait_ge(turned[g], ITERS)
                act.copy(yt[:, g % RING, :, :, :], pt[:, g % RING, :]).then_inc(yt_done[g], 1)

        def pe_stream(pe, i, last):
            def turn(g):
                q, here = last_user(g)
                pe.wait_ge(y_done[g], i * 2)
                if here or some(i - 1):
                    pe.wait_ge(yt_done[q], i if here else i - 1)
                for r in range(2):
                    for k in range(KD):
                        mm = pe.transpose(pt[:, g % RING, (r * KD + k) * P:(r * KD + k + 1) * P],
                                          gg[:, g, r, k * P:(k + 1) * P], ident[:, :])
                mm.then_inc(turned[g], 1)

            def product(g):
                q, here = last_user(g)
                pe.wait_ge(yt_done[g], i)
                if here and last:
                    pe.wait_ge(out_done, q + 1)
                elif here:
                    pe.wait_ge(g_done[q], i + 1)
                else:
                    pe.wait_ge(g_done[q], i)
                for r in range(2):
                    out = pm[:, g % RING, r * D:(r + 1) * D]
                    for k in range(KD):
                        pe.matmul(out, yt[:, g % RING, r, k, :], wl[:, k, :], start=(k == 0), stop=False)
                    mm = pe.matmul(out, ones3[:, :], crow[:, :], start=False, stop=True)
                mm.then_inc(h_mm[g], 1)
            for g in range(NPAIR + 1):
                if g < NPAIR:
                    turn(g)
                if g:
                    product(g - 1)

        @block.tensor
        def _(pe):
            pe.wait_ge(w_in, 64)
            for k in range(KD):
                for j in range(KD):
                    mm = pe.transpose(pt[:, 0, (k * KD + j) * P:(k * KD + j + 1) * P],
                                      wn[:, j, k * P:(k + 1) * P], ident[:, :])
            mm.then_inc(w_ps, 1)
            pe.wait_ge(w_sb, 1)
            pe.wait_ge(w_scaled, KD)
            for k in range(KD):
                mm = pe.matmul(pm[0:3, 0, 0:D], lb3[:, k, :], wt[:, k, :, :].rearrange("p j o -> p (j o)"),
                               start=(k == 0), stop=(k == KD - 1))
            mm.then_inc(c_mm, 1)
            pe.wait_ge(w_scaled, 2 * KD)
            pe.wait_ge(c_done, 1)
            pe_stream(pe, 1, False)
            with pe.Fori(2, ITERS) as i:
                pe_stream(pe, i, False)
            pe_stream(pe, ITERS, True)


def build(nc, io):
    with ExitStack() as whole:
        def buffers(ctx, **shapes):
            return {n: ctx.enter_context(nc.sbuf_tensor(n, s[0], s[1] if len(s) > 1 else F32))
                    for n, s in shapes.items()}

        keep = buffers(whole, X=([P, NT, D],), ident=([P, P],), neg_half=([P, NT],))
        for name, rows in (("XD", XTILES * P), ("YD", XTILES * P), ("OD", NT * P)):
            keep[name] = nc.dram_tensor(name, (rows, D), F32).ap()
        with ExitStack() as part:
            layer0 = buffers(part, V=([P, NT, H, VW],), F1=([P, H, N],), F2=([P, 2, NT, H],))
            layer0_prepare(nc, io, {**keep, **layer0})
            layer0_attention(nc, io, {**keep, **layer0})
        with ExitStack() as part:
            moe = buffers(part, XF=([P, NT, D],), POSI=([P, TOPK * NT], U32), GW=([P, TOPK, NT],),
                          GD=([P, NT, E],), TE=([1, XTILES], I32))
            with ExitStack() as weights:
                moe.update(buffers(weights, W1=([P, E, KD, F],), W2=([P, E, FB, D],)),
                           w_in=weights.enter_context(nc.semaphore("expert_weights_in")))
                moe_route(nc, io, keep, moe)
                moe_experts(nc, io, keep, moe)
            moe_combine(nc, io, keep, moe)
        with ExitStack() as part:
            layer1 = buffers(part, V1=([P, NT, H, VW],), QT=([P, H, NT * P], F16), KH=([P, H, N], F16),
                             KL=([P, H, N], F16))
            layer1_prepare(nc, io, {**keep, "V": layer1["V1"]}, layer1)
            layer1_attention(nc, io, {**keep, "V": layer1["V1"]}, layer1)
        layer1_project(nc, io, keep)
        layer1_ffn(nc, io, keep)


_INS = ["x", "adj", "L0_gnn_weight", "L0_gnn_weight_u", "L0_gnn_weight_v", "L0_gnn_bias", "L0_gnn_proj_w",
        "L0_gnn_proj_b", "L0_ffn_gate_w", "L0_ffn_gate_b", "L0_ffn_w1", "L0_ffn_b1", "L0_ffn_w2", "L0_ffn_b2",
        "L0_ffn_gamma", "L0_ffn_beta", "L1_gnn_Wqkv", "L1_gnn_bqkv", "L1_gnn_Wout", "L1_gnn_bout",
        "L1_gnn_graph_bias", "L1_ffn_ln_w", "L1_ffn_ln_b", "L1_ffn_W", "L1_ffn_b"]


def kernel(**inputs):
    import numpy as _np
    import concourse.bacc as _bacc
    from concourse import mybir as _mybir
    from concourse.bass_utils import run_bass_kernel_spmd as _run

    nc = _bacc.Bacc("TRN2", target_bir_lowering=False, num_devices=1)
    arrays, io = {}, {}
    for name in _INS:
        a = _np.ascontiguousarray(inputs[name])
        arrays[f"in_{name}"] = a
        io[name] = nc.dram_tensor(f"in_{name}", a.shape, _mybir.dt.from_np(a.dtype), kind="ExternalInput").ap()
    io["out"] = nc.dram_tensor("out", (N, D), _mybir.dt.float32, kind="ExternalOutput").ap()
    build(nc, io)
    r = _run(nc, [arrays], core_ids=[0])
    return r.results[0]["out"]
```

```python
from contextlib import ExitStack

import concourse.bass as bass
from concourse import mybir

ALU = mybir.AluOpType
ACT = mybir.ActivationFunctionType
AX = mybir.AxisListType
F32 = mybir.dt.float32
F16 = mybir.dt.float16
BF16 = mybir.dt.bfloat16
U32 = mybir.dt.uint32
I32 = mybir.dt.int32

P = 128
N = 2708
D = 256
KD = D // P
NT = -(-N // P)
LAST = N - P
OVER = P * NT - N
H, HD = 4, 64
VW = HD + 1
NPAIR = NT // 2
BATCHES = [(a, min(a + 3, NPAIR)) for a in range(0, NPAIR, 3)]
GRP = 4
NG = -(-NT // GRP)
E, F, TOPK = 16, 512, 2
FB = F // P
XTILES = (TOPK * NT * P + E * (P - 1)) // P + 1
XTILES += XTILES % 2
ITERS = 30
EPS = 1e-5
SLOPE = 0.2
BIG = 3e38
FLOOR = -1e37
MASKED = -1e9


class Phase:

    def __init__(self, nc, name):
        self.nc, self.name, self.ctx = nc, name, ExitStack()
        self.counters = []

    def __enter__(self):
        self.ctx.__enter__()
        return self

    def __exit__(self, *a):
        done = self.ctx.__exit__(*a)
        self.nc.clear_and_free_semaphores(self.counters)
        self.nc.all_engine_barrier()
        return done

    def sb(self, name, shape, dt=F32):
        return self.ctx.enter_context(self.nc.sbuf_tensor(f"{self.name}_{name}", shape, dt))

    def ps(self, name, shape, dt=F32):
        return self.ctx.enter_context(self.nc.psum_tensor(f"{self.name}_{name}", shape, dt))

    def sem(self, name):
        self.counters.append(self.nc.alloc_semaphore(f"{self.name}_{name}"))
        return self.counters[-1]

    def sems(self, names):
        return [self.sem(n) for n in names.split()]

    def block(self):
        return self.ctx.enter_context(self.nc.Block())


def some(n):
    return not isinstance(n, int) or n > 0


def bcast_rows(ap, rows):
    return ap.rearrange("(a d) -> a d", a=1).to_broadcast([rows, ap.shape[0]])


def row_moments(dve, st, mom, s0, s1, chain, base):
    n = slice(s0, s1)
    even_m, even_q, odd_m, odd_q = (st[:, n, j] for j in (1, 2, 4, 5))
    dve.tensor_tensor(mom[:, 0, n], even_m, odd_m, ALU.add)
    dve.tensor_tensor(mom[:, 2, n], even_m, odd_m, ALU.subtract).then_inc(chain, 1)
    dve.tensor_tensor(mom[:, 3, n], even_q, odd_q, ALU.add).then_inc(chain, 1)
    dve.wait_ge(chain, base + 1)
    dve.scalar_tensor_tensor(mom[:, 4, n], mom[:, 2, n], 0.25, mom[:, 2, n],
                             ALU.mult, ALU.mult).then_inc(chain, 1)
    dve.wait_ge(chain, base + 3)
    return dve.scalar_tensor_tensor(mom[:, 1, n], mom[:, 3, n], 1.0 / D, mom[:, 4, n], ALU.mult, ALU.add)


def inverse_deviation(pool, mom, rs, neg_half, s0, s1, chain, base):
    n = slice(s0, s1)
    pool.tensor_scalar(rs[:, 2, n], mom[:, 1, n], EPS, None, ALU.add).then_inc(chain, 1)
    pool.tensor_scalar(rs[:, 3, n], mom[:, 0, n], -0.5, None, ALU.mult).then_inc(chain, 1)
    pool.wait_ge(chain, base + 1)
    pool.tensor_tensor(rs[:, 0, n], rs[:, 2, n], neg_half[:, n], ALU.pow).then_inc(chain, 1)
    pool.wait_ge(chain, base + 3)
    return pool.tensor_tensor(rs[:, 1, n], rs[:, 3, n], rs[:, 0, n], ALU.mult)


def standard_rows(eng, out, x, rs, t):
    return eng.tensor_scalar(out, x, rs[:, 0, bass.ds(t, 1)], rs[:, 1, bass.ds(t, 1)], ALU.mult, ALU.add)


def first_adj(sp, io, adj, adj_in):
    for b in range(2):
        sp.dma_start(adj[:, b, :], io["adj"][b * P:(b + 1) * P, :]).then_inc(adj_in[b], 16)


def slot_pairs(eng, body):
    with eng.Fori(0, NPAIR - 1) as i:
        for b in range(2):
            body(i, b)
    for b in range(2):
        body(NPAIR - 1, b)


def slot_moments(dve, x, st, mom, stats, folded, moments, arrived=None):
    for k, (a, end) in enumerate(BATCHES):
        if arrived:
            dve.wait_ge(*arrived[k])
        with dve.Fori(2 * a, 2 * end) as t:
            dve.bn_stats(st[:, bass.ds(t, 1), :], x[:, bass.ds(t, 1), :]).then_inc(stats, 1)
        dve.wait_ge(stats, 2 * end)
        row_moments(dve, st, mom, 2 * a, 2 * end, folded, 3 * k).then_inc(moments, 1)


def slot_deviation(pool, t, mom, rs, neg_half, moments, chain, inv):
    for k, (a, end) in enumerate(BATCHES):
        if t == 2 * a:
            pool.wait_ge(moments, k + 1)
            inverse_deviation(pool, mom, rs, neg_half, 2 * a, 2 * end, chain, 3 * k).then_inc(inv, 1)
            pool.wait_ge(inv, k + 1)


def layer0_prepare(nc, io, keep):
    X, V, F1, F2, ident, neg_half = (keep[n] for n in ("X", "V", "F1", "F2", "ident", "neg_half"))
    with Phase(nc, "p0") as ph:
        w = ph.sb("w", [P, KD, D + H])
        pw = ph.sb("pw", [P, KD, D])
        pwt = ph.sb("pwt", [P, KD, KD, P])
        uv = ph.sb("uv", [P, 2, D])
        prod = ph.sb("prod", [P, 2, KD, D])
        wuv = ph.sb("wuv", [P, 2, KD, H])
        wub = ph.sb("wub", [P, KD, H, P])
        bias = ph.sb("bias", [P, 3, D])
        zeros = ph.sb("zeros", [P, D])
        ones = ph.sb("ones", [P, P])
        rows_kept = ph.sb("rows_kept", [P, 1])
        st = ph.sb("st", [P, NT, 6])
        mom = ph.sb("mom", [P, 5, NT])
        rs = ph.sb("rs", [P, 4, NT])
        xn = ph.sb("xn", [P, 2, D])
        xt = ph.sb("xt", [P, 2, KD, P])
        pt = ph.ps("pt", [P, 2, 512])
        pf = ph.ps("pf", [P, 2, 512])
        pv = ph.ps("pv", [P, 2, 512])
        pp = ph.ps("pp", [P, 2, 512])
        x_in = ph.sems(" ".join(f"x_in{k}" for k in range(len(BATCHES))))
        (w_in, uv_in, cleared, consts, stats, moments, inv, pchain, folded, wub_done, pwt_ps, pwt_sb,
         bsum, xd_zero, prods, masked) = ph.sems(
            "w_in uv_in cleared consts stats moments inv pchain folded wub_done pwt_ps pwt_sb "
            "bsum xd_zero prods masked")
        xn_done, turned, xt_done, f_mm, v_mm, p_mm, f_out, v_out, biased, x_out = (
            ph.sems(f"{n}0 {n}1") for n in
            "xn_done turned xt_done f_mm v_mm p_mm f_out v_out biased x_out".split())
        block = ph.block()

        @block.sync
        def _(sp):
            sp.dma_start(w[:, :, 0:D], io["L0_gnn_weight"].rearrange("(k p) o -> p k o", p=P)).then_inc(uv_in, 16)
            for j, name in enumerate(("L0_gnn_weight_u", "L0_gnn_weight_v")):
                sp.dma_start(uv[:, j, :], bcast_rows(io[name].rearrange("h o a -> (h o a)"), P)).then_inc(uv_in, 16)
            for k, (a, end) in enumerate(BATCHES):
                s0, s1 = 2 * a, min(2 * end, NT - 1)
                sp.dma_start(X[:, s0:s1, :], io["x"][P * s0:P * s1, :].rearrange("(t p) d -> p t d", p=P)
                             ).then_inc(x_in[k], 16)
            sp.dma_start(X[:, NT - 1, :], io["x"][LAST:N, :]).then_inc(x_in[-1], 16)
            sp.dma_start(pw[:, :, :], io["L0_gnn_proj_w"].rearrange("(k p) o -> p k o", p=P)).then_inc(w_in, 16)
            sp.dma_start(bias[:, 0, :], io["L0_gnn_bias"].to_broadcast([P, D])).then_inc(w_in, 16)
            sp.dma_start(bias[:, 1, :], bcast_rows(io["L0_gnn_proj_b"], P)).then_inc(w_in, 16)
            first_adj(sp, io, keep["ADJ0"], keep["adj_in"])
            sp.wait_ge(cleared, 2)
            sp.dma_start(keep["XD"].rearrange("(j p) d -> p j d", p=P),
                         zeros[:, :].rearrange("p (a d) -> p a d", a=1).to_broadcast([P, XTILES, D])
                         ).then_inc(xd_zero, 16)
            sp.wait_ge(xd_zero, 16)

        @block.gpsimd
        def _(pool):
            pool.memset(ident[:, :], 0.0).then_inc(cleared, 1)
            pool.memset(zeros[:, :], 0.0).then_inc(cleared, 1)
            pool.memset(rows_kept[:, :], 1.0).then_inc(cleared, 1)
            pool.memset(neg_half[:, :], -0.5).then_inc(cleared, 1)
            pool.wait_ge(cleared, 4)
            pool.affine_select(out=ident[:, :], in_=ident[:, :], compare_op=ALU.not_equal, fill=1.0, base=0,
                               pattern=[[-1, P]], channel_multiplier=1).then_inc(consts, 1)
            pool.affine_select(out=rows_kept[:, :], in_=rows_kept[:, :], compare_op=ALU.is_ge, fill=0.0,
                               base=-OVER, pattern=[[0, 1]], channel_multiplier=1).then_inc(consts, 1)
            pool.wait_ge(w_in, 48)
            pool.tensor_tensor(bias[:, 2, :], bias[:, 0, :], bias[:, 1, :], ALU.add).then_inc(bsum, 1)
            pool.wait_ge(bsum, 1)

            def normal(i, b):
                t = i * 2 + b
                slot_deviation(pool, t, mom, rs, neg_half, moments, pchain, inv)
                if some(i):
                    pool.wait_ge(turned[b], i)
                xs = X[:, bass.ds(t, 1), :]
                standard_rows(pool, xn[:, b:b + 1, :], xs, rs, t).then_inc(xn_done[b], 1)
                pool.wait_ge(xn_done[b], i + 1)
                pool.tensor_tensor(xs, xs, bias[:, 2:3, :], ALU.add).then_inc(biased[b], 1)
            for t in range(NT):
                normal(t // 2, t % 2)

        @block.vector
        def _(dve):
            dve.memset(ones[:, :], 1.0).then_inc(prods, 1)
            dve.memset(V[:, :, :, HD:VW], 1.0)
            dve.wait_ge(uv_in, 48)
            for j in range(2):
                for k in range(KD):
                    dve.tensor_tensor(prod[:, j, k, :], w[:, k, 0:D], uv[:, j, :], ALU.mult).then_inc(prods, 1)
            dve.wait_ge(prods, 5)
            for j in range(2):
                dve.tensor_reduce(wuv[:, j, :, :], prod[:, j, :, :].rearrange("p k (h o) -> p k h o", h=H),
                                  AX.X, ALU.add).then_inc(prods, 1)
            dve.wait_ge(prods, 7)
            dve.tensor_copy(w[:, :, D:D + H], wuv[:, 1, :, :]).then_inc(wub_done, 1)
            for k in range(KD):
                for h in range(H):
                    dve.tensor_scalar(wub[:, k, h, :], ones[:, :], wuv[:, 0, k, h:h + 1], None,
                                      ALU.mult).then_inc(wub_done, 1)

            slot_moments(dve, X, st, mom, stats, folded, moments,
                         [(s, 32 if s is x_in[-1] else 16) for s in x_in])

            def results(i, b):
                t = i * 2 + b
                dve.wait_ge(v_mm[b], i + 1)
                dve.tensor_copy(V[:, bass.ds(t, 1), :, 0:HD],
                                pv[:, b:b + 1, 0:D].rearrange("p a (h o) -> p a h o", h=H)).then_inc(v_out[b], 1)
                dve.tensor_copy(F2[:, 0, bass.ds(t, 1), :], pv[:, b:b + 1, D:D + H]).then_inc(v_out[b], 1)
                dve.wait_ge(p_mm[b], i + 1)
                dve.wait_ge(biased[b], i + 1)
                xs = X[:, bass.ds(t, 1), :]
                dve.tensor_tensor(xs, pp[:, b:b + 1, 0:D], xs, ALU.add).then_inc(x_out[b], 1)
            slot_pairs(dve, results)
            for b in range(2):
                dve.wait_ge(v_out[b], 2 * NPAIR)
            dve.wait_ge(consts, 2)
            dve.tensor_scalar(V[:, NT - 1, :, :], V[:, NT - 1, :, :], rows_kept[:, :], None, ALU.mult).then_inc(masked, 1)
            dve.tensor_scalar(F2[:, 1, :, :], F2[:, 0, :, :], SLOPE, None, ALU.mult).then_inc(masked, 1)
            dve.wait_ge(masked, 2)

        @block.tensor
        def _(pe):
            pe.wait_ge(w_in, 48)
            pe.wait_ge(consts, 1)
            for k in range(KD):
                for j in range(KD):
                    mm = pe.transpose(pf[:, 0, (k * KD + j) * P:(k * KD + j + 1) * P],
                                      pw[:, j, k * P:(k + 1) * P], ident[:, :])
            mm.then_inc(pwt_ps, 1)
            pe.wait_ge(pwt_sb, 1)
            pe.wait_ge(wub_done, 1 + KD * H)

            def turn(i, b):
                pe.wait_ge(xn_done[b], i + 1)
                if some(i):
                    pe.wait_ge(xt_done[b], i)
                for k in range(KD):
                    mm = pe.transpose(pt[:, b, k * P:(k + 1) * P], xn[:, b, k * P:(k + 1) * P], ident[:, :])
                mm.then_inc(turned[b], 1)

            def product(i, b):
                pe.wait_ge(xt_done[b], i + 1)
                if some(i):
                    pe.wait_ge(f_out[b], i)
                if some(i * 2):
                    pe.wait_ge(v_out[b], i * 2)
                if some(i):
                    pe.wait_ge(x_out[b], i)
                for h in range(H):
                    for k in range(KD):
                        mm = pe.matmul(pf[:, b, h * P:(h + 1) * P], wub[:, k, h, :], xt[:, b, k, :],
                                       start=(k == 0), stop=(k == KD - 1))
                mm.then_inc(f_mm[b], 1)
                for k in range(KD):
                    mm = pe.matmul(pv[:, b, 0:D + H], xt[:, b, k, :], w[:, k, :],
                                   start=(k == 0), stop=(k == KD - 1))
                mm.then_inc(v_mm[b], 1)
                for k in range(KD):
                    mm = pe.matmul(pp[:, b, 0:D], xt[:, b, k, :], pwt[:, k, :, :],
                                   start=(k == 0), stop=(k == KD - 1))
                mm.then_inc(p_mm[b], 1)

            turn(0, 0)
            def pair(i):
                turn(i, 1)
                product(i, 0)
                turn(i + 1, 0)
                product(i, 1)
            pair(0)
            with pe.Fori(1, NPAIR - 1) as i:
                pair(i)
            turn(NPAIR - 1, 1)
            product(NPAIR - 1, 0)
            product(NPAIR - 1, 1)

        @block.scalar
        def _(act):
            act.wait_ge(pwt_ps, 1)
            act.copy(pwt[:, :, :, :], pf[:, 0, :]).then_inc(pwt_sb, 1)
            act.wait_ge(pwt_sb, 1)

            def turned_out(i, b):
                act.wait_ge(turned[b], i + 1)
                act.copy(xt[:, b, :, :], pt[:, b, 0:D]).then_inc(xt_done[b], 1)

            def f1_out(i, b):
                act.wait_ge(f_mm[b], i + 1)
                col = LAST if isinstance(i, int) and i * 2 + b == NT - 1 else (i * 2 + b) * P
                act.copy(F1[:, :, bass.ds(col, P)],
                         pf[:, b, :].rearrange("p (h n) -> p h n", h=H)).then_inc(f_out[b], 1)

            turned_out(0, 0)
            with act.Fori(0, NPAIR - 1) as i:
                turned_out(i, 1)
                f1_out(i, 0)
                turned_out(i + 1, 0)
                f1_out(i, 1)
            turned_out(NPAIR - 1, 1)
            f1_out(NPAIR - 1, 0)
            act.wait_ge(f_out[0], NPAIR)
            f1_out(NPAIR - 1, 1)


def later(unit, k):
    i, b, h = unit
    n = b * H + h + k
    i = i + n // (2 * H)
    if isinstance(i, int) and not 0 <= i < NPAIR:
        return None
    return i, n % (2 * H) // H, n % H


def over_units(eng, step):
    def pair(i):
        for b in range(2):
            for h in range(H):
                step((i, b, h))
    pair(0)
    with eng.Fori(1, NPAIR - 1) as i:
        pair(i)
    pair(NPAIR - 1)


def layer0_attention(nc, io, keep):
    X, V, F1, F2, ident, adj, adj_in = (keep[n] for n in ("X", "V", "F1", "F2", "ident", "ADJ0", "adj_in"))
    with Phase(nc, "a0") as ph:
        off = ph.sb("off", [P, 2, N])
        low = ph.sb("low", [P, N])
        lg = ph.sb("lg", [P, H, N])
        wt = ph.sb("wt", [P, NT, P])
        mx = ph.sb("mx", [P, H, 2])
        den = ph.sb("den", [P, 2, 2, H])
        res = ph.sb("res", [P, 2, H, HD])
        tp = ph.ps("tp", [P, NG, 512])
        po = ph.ps("po", [P, 2, 512])
        off_done, heads_in, heads_out, d_ok, r_ok, n_ok = (
            ph.sems(f"{n}0 {n}1") for n in "off_done heads_in heads_out d_ok r_ok n_ok".split())
        low_done, lrelu, times, masked, neg_max, exp_done = (
            ph.sems(" ".join(f"{n}{h}" for h in range(H))) for n in
            "low_done lrelu times masked neg_max exp_done".split())
        turned = ph.sems(" ".join(f"turned{g}" for g in range(NG)))
        copied = ph.sems(" ".join(f"copied{g}" for g in range(NG)))
        block = ph.block()
        by_dve = (NG - 1,)

        def tiles(unit):
            i, b, h = unit
            return i * 2 + (b + 1)

        def units(unit):
            i, b, h = unit
            return i * (2 * H) + (b * H + h + 1)

        def copies(eng, copy, unit, groups):
            for g in groups:
                n = min(GRP, NT - GRP * g)
                eng.wait_ge(turned[g], units(unit))
                copy(wt[:, GRP * g:GRP * g + n, :], tp[:, g, 0:n * P]).then_inc(copied[g], 1)

        @block.sync
        def _(sp):
            with sp.Fori(1, NPAIR - 1) as i:
                for b in range(2):
                    sp.wait_ge(masked[H - 1], i * 2 + (b - 1))
                    sp.dma_start(adj[:, b, :], io["adj"][bass.ds((i * 2 + b) * P, P), :]).then_inc(adj_in[b], 16)
            for b in range(2):
                sp.wait_ge(masked[H - 1], (NPAIR - 1) * 2 + b - 1)
                row = (NT - 2) * P if b == 0 else LAST
                sp.dma_start(adj[:, b, :], io["adj"][row:row + P, :]).then_inc(adj_in[b], 16)

        @block.gpsimd
        def _(pool):
            def step(unit):
                i, b, h = unit
                pool.wait_ge(lrelu[h], tiles(unit))
                if h == 0:
                    pool.wait_ge(adj_in[b], i * 16 + 16)
                pool.nop(nofuse=True)
                pool.tensor_tensor(lg[:, h, :], lg[:, h, :], adj[:, b, :], ALU.mult).then_inc(times[h], 1)
            over_units(pool, step)

        @block.scalar
        def _(act):
            def low_part(unit):
                i, b, h = unit
                if later(unit, -1):
                    act.wait_ge(lrelu[later(unit, -1)[2]], tiles(later(unit, -1)))
                act.activation(low[:, :], F1[:, h, :], ACT.Identity, scale=SLOPE,
                               bias=F2[:, 1, bass.ds(i * 2 + b, 1), h]).then_inc(low_done[h], 1)

            def exp_part(unit):
                h = unit[2]
                act.wait_ge(neg_max[h], tiles(unit))
                act.activation(lg[:, h, :], lg[:, h, :], ACT.Exp, bias=mx[:, h, 1:2]).then_inc(exp_done[h], 1)

            def step(unit):
                before, after = later(unit, -1), later(unit, 3)
                if before:
                    exp_part(before)
                if after:
                    low_part(after)
                if before:
                    copies(act, act.copy, before, range(NG - len(by_dve)))
            low_part((0, 0, 0))
            low_part((0, 0, 1))
            low_part((0, 0, 2))
            over_units(act, step)
            last = (NPAIR - 1, 1, H - 1)
            exp_part(last)
            copies(act, act.copy, last, range(NG - len(by_dve)))

        @block.vector
        def _(dve):
            def leaky(unit):
                i, b, h = unit
                dve.wait_ge(low_done[h], tiles(unit))
                dve.scalar_tensor_tensor(lg[:, h, :], F1[:, h, :], F2[:, 0, bass.ds(i * 2 + b, 1), h],
                                         low[:, :], ALU.add, ALU.max).then_inc(lrelu[h], 1)

            def off_tile(i, b):
                dve.wait_ge(adj_in[b], i * 16 + 16)
                dve.tensor_scalar(off[:, b, :], adj[:, b, :], 0.0, -BIG, ALU.is_equal,
                                  ALU.mult).then_inc(off_done[b], 1)

            def mask(unit):
                i, b, h = unit
                if h == 0:
                    dve.wait_ge(off_done[b], i + 1)
                dve.wait_ge(times[h], tiles(unit))
                dve.nop(nofuse=True)
                dve.tensor_tensor_reduce(lg[:, h, :], lg[:, h, :], off[:, b, :], 1.0, -BIG, ALU.add, ALU.max,
                                         mx[:, h, 0:1]).then_inc(masked[h], 1)
                dve.wait_ge(masked[h], tiles(unit))
                dve.tensor_scalar(mx[:, h, 1:2], mx[:, h, 0:1], FLOOR, -1.0, ALU.max,
                                  ALU.mult).then_inc(neg_max[h], 1)

            def finish(i, b):
                sums = po[:, b, 0:H * VW].rearrange("p (h v) -> p h v", h=H)
                dve.wait_ge(heads_in[b], i + 1)
                dve.tensor_scalar(den[:, b, 0, :], sums[:, :, HD], 1e-30, None, ALU.max).then_inc(d_ok[b], 1)
                dve.wait_ge(d_ok[b], i + 1)
                dve.reciprocal(den[:, b, 1, :], den[:, b, 0, :]).then_inc(r_ok[b], 1)
                dve.wait_ge(r_ok[b], i + 1)
                dve.tensor_tensor(res[:, b, :, :], sums[:, :, 0:HD],
                                  den[:, b, 1, :].rearrange("p (h a) -> p h a", a=1).to_broadcast([P, H, HD]),
                                  ALU.mult).then_inc(n_ok[b], 1)
                dve.wait_ge(n_ok[b], i + 1)
                xs = X[:, bass.ds(i * 2 + b, 1), :]
                dve.tensor_tensor(xs, xs, res[:, b:b + 1, :, :].rearrange("p a h o -> p a (h o)"),
                                  ALU.add).then_inc(heads_out[b], 1)

            def step(unit):
                if later(unit, 2):
                    leaky(later(unit, 2))
                mask(unit)
                if later(unit, -1):
                    copies(dve, dve.tensor_copy, later(unit, -1), by_dve)
                if unit[2] == 1 and later(unit, -H):
                    finish(*later(unit, -H)[:2])
                if unit[2] == 2 and later(unit, H):
                    off_tile(*later(unit, H)[:2])
            off_tile(0, 0)
            leaky((0, 0, 0))
            leaky((0, 0, 1))
            over_units(dve, step)
            copies(dve, dve.tensor_copy, (NPAIR - 1, 1, H - 1), by_dve)
            finish(NPAIR - 1, 1)

        @block.tensor
        def _(pe):
            def step(unit):
                i, b, h = unit
                pe.wait_ge(exp_done[h], tiles(unit))
                for g in range(NG):
                    for j in range(GRP * g, min(GRP * g + GRP, NT)):
                        col = min(j * P, LAST)
                        mm = pe.transpose(tp[:, g, (j % GRP) * P:(j % GRP + 1) * P],
                                          lg[:, h, col:col + P], ident[:, :])
                    mm.then_inc(turned[g], 1)
                if h == 0 and some(i):
                    pe.wait_ge(heads_out[b], i)
                for g in range(NG):
                    pe.wait_ge(copied[g], units(unit))
                    for j in range(GRP * g, min(GRP * g + GRP, NT)):
                        mm = pe.matmul(po[:, b, h * VW:(h + 1) * VW], wt[:, j, :], V[:, j, h, :],
                                       start=(j == 0), stop=(j == NT - 1))
                if h == H - 1:
                    mm.then_inc(heads_in[b], 1)
            over_units(pe, step)


def layer1_prepare(nc, io, keep, layer1):
    X, V, ident, neg_half = (keep[n] for n in ("X", "V", "ident", "neg_half"))
    QT, KH, KL = (layer1[n] for n in ("QT", "KH", "KL"))
    with Phase(nc, "p1") as ph:
        wqkv = ph.sb("wqkv", [P, KD, 3 * D])
        wqk = ph.sb("wqk", [P, KD, 2, H, 2, HD])
        bqk = ph.sb("bqk", [P, 2, H])
        bv = ph.sb("bv", [P, D])
        rows_kept = ph.sb("rows_kept", [P, 1])
        st = ph.sb("st", [P, NT, 6])
        mom = ph.sb("mom", [P, 5, NT])
        rs = ph.sb("rs", [P, 4, NT])
        xn = ph.sb("xn", [P, 2, D])
        xt = ph.sb("xt", [P, 2, KD, P])
        full = ph.sb("full", [P, 2, 2, H, P])
        pt = ph.ps("pt", [P, 2, 512])
        pq = ph.ps("pq", [P, 2, 512])
        pk = ph.ps("pk", [P, 2, 512])
        pv = ph.ps("pv", [P, 2, 512])
        (w_in, b_in, scaled, kept0, kept, stats, moments, inv, pchain, folded, doubled, masked) = ph.sems(
            "w_in b_in scaled kept0 kept stats moments inv pchain folded doubled masked")
        xn_done, turned, xt_done, q_mm, k_mm, v_mm, q_full, k_full, high_done, low_done, v_out = (
            ph.sems(f"{n}0 {n}1") for n in
            "xn_done turned xt_done q_mm k_mm v_mm q_full k_full high_done low_done v_out".split())
        block = ph.block()

        @block.sync
        def _(sp):
            sp.dma_start(wqkv[:, :, :], io["L1_gnn_Wqkv"].rearrange("(k p) o -> p k o", p=P)).then_inc(w_in, 16)
            sp.dma_start(bv[:, :], bcast_rows(io["L1_gnn_bqkv"][2 * D:3 * D], P)).then_inc(b_in, 16)
            with nc.allow_non_contiguous_dma(reason="a bias column per head"):
                for r in range(2):
                    sp.dma_start(bqk[r * HD:(r + 1) * HD, :, :],
                                 io["L1_gnn_bqkv"][0:2 * D].rearrange("(j h o) -> o j h", j=2, h=H)
                                 ).then_inc(b_in, 16)
            first_adj(sp, io, layer1["ADJ1"], layer1["adj_in"])

        @block.gpsimd
        def _(pool):
            pool.memset(rows_kept[:, :], 1.0).then_inc(kept0, 1)
            pool.wait_ge(kept0, 1)
            pool.affine_select(out=rows_kept[:, :], in_=rows_kept[:, :], compare_op=ALU.is_ge, fill=0.0,
                               base=-OVER, pattern=[[0, 1]], channel_multiplier=1).then_inc(kept, 1)

            def normal(i, b):
                slot_deviation(pool, i * 2 + b, mom, rs, neg_half, moments, pchain, inv)
                if some(i):
                    pool.wait_ge(turned[b], i)
                standard_rows(pool, xn[:, b:b + 1, :], X[:, bass.ds(i * 2 + b, 1), :], rs,
                              i * 2 + b).then_inc(xn_done[b], 1)
            for t in range(NT):
                normal(t // 2, t % 2)

        @block.vector
        def _(dve):
            dve.memset(V[:, :, :, HD:VW], 1.0)
            slot_moments(dve, X, st, mom, stats, folded, moments)
            dve.wait_ge(b_in, 48)

            def results(i, b):
                t = i * 2 + b
                last = isinstance(i, int) and t == NT - 1
                col = LAST if last else t * P
                dve.wait_ge(q_full[b], i * H + H)
                dve.wait_ge(k_full[b], i * H + H)
                dve.tensor_copy(QT[:, :, bass.ds(t * P, P)], full[:, b, 0, :, :]).then_inc(high_done[b], 1)
                if last:
                    dve.wait_ge(low_done[0], 2 * NPAIR)
                dve.tensor_copy(KH[:, :, bass.ds(col, P)], full[:, b, 1, :, :]).then_inc(high_done[b], 1)
                dve.wait_ge(v_mm[b], i + 1)
                dve.tensor_tensor(V[:, bass.ds(t, 1), :, 0:HD],
                                  pv[:, b:b + 1, 0:D].rearrange("p a (h o) -> p a h o", h=H),
                                  bv[:, :].rearrange("p (a h o) -> p a h o", a=1, h=H),
                                  ALU.add).then_inc(v_out[b], 1)
                dve.wait_ge(high_done[b], i * 2 + 2)
                lows = slice(HD, P)
                dve.tensor_tensor(QT[lows, :, bass.ds(t * P, P)], full[lows, b, 0, :, :],
                                  QT[lows, :, bass.ds(t * P, P)], ALU.subtract).then_inc(low_done[b], 1)
                dve.tensor_tensor(KL[:, :, bass.ds(col, P)], full[:, b, 1, :, :], KH[:, :, bass.ds(col, P)],
                                  ALU.subtract).then_inc(low_done[b], 1)
            slot_pairs(dve, results)
            for b in range(2):
                dve.wait_ge(v_out[b], NPAIR)
            dve.wait_ge(kept, 1)
            dve.tensor_scalar(V[:, NT - 1, :, :], V[:, NT - 1, :, :], rows_kept[:, :], None,
                              ALU.mult).then_inc(masked, 1)
            dve.wait_ge(masked, 1)

        @block.scalar
        def _(act):
            act.wait_ge(w_in, 16)
            for j in range(2):
                for r in range(2):
                    for k in range(KD):
                        act.copy(wqk[:, k, j, :, r, :], wqkv[:, k, j * D:(j + 1) * D].rearrange(
                            "p (h o) -> p h o", h=H)).then_inc(doubled, 1)
            act.wait_ge(b_in, 48)
            act.activation(bqk[:, 0, :], bqk[:, 0, :], ACT.Identity, scale=HD ** -0.5).then_inc(scaled, 1)
            act.wait_ge(scaled, 1)

            def turned_out(i, b):
                act.wait_ge(turned[b], i + 1)
                act.copy(xt[:, b, :, :], pt[:, b, 0:D]).then_inc(xt_done[b], 1)

            def full_out(i, b):
                if some(i * 2):
                    act.wait_ge(low_done[b], i * 2)
                for j, (done, mm, src, scale) in enumerate(((q_full, q_mm, pq, HD ** -0.5),
                                                            (k_full, k_mm, pk, 1.0))):
                    act.wait_ge(mm[b], i + 1)
                    for h in range(H):
                        act.activation(full[:, b, j, h, :], src[:, b, h * P:(h + 1) * P], ACT.Identity,
                                       scale=scale, bias=bqk[:, j, h:h + 1]).then_inc(done[b], 1)

            turned_out(0, 0)
            def pair(i):
                turned_out(i, 1)
                full_out(i, 0)
                turned_out(i + 1, 0)
                full_out(i, 1)
            pair(0)
            with act.Fori(1, NPAIR - 1) as i:
                pair(i)
            turned_out(NPAIR - 1, 1)
            full_out(NPAIR - 1, 0)
            full_out(NPAIR - 1, 1)

        @block.tensor
        def _(pe):
            pe.wait_ge(w_in, 16)
            pe.wait_ge(doubled, 8)

            def turn(i, b):
                pe.wait_ge(xn_done[b], i + 1)
                if some(i):
                    pe.wait_ge(xt_done[b], i)
                for k in range(KD):
                    mm = pe.transpose(pt[:, b, k * P:(k + 1) * P], xn[:, b, k * P:(k + 1) * P], ident[:, :])
                mm.then_inc(turned[b], 1)

            def product(i, b):
                pe.wait_ge(xt_done[b], i + 1)
                for j, (mm_done, out_done, dst) in enumerate(((q_mm, q_full, pq), (k_mm, k_full, pk))):
                    if some(i * H):
                        pe.wait_ge(out_done[b], i * H)
                    for h in range(H):
                        for k in range(KD):
                            mm = pe.matmul(dst[:, b, h * P:(h + 1) * P],
                                           wqk[:, k, j, h, :, :].rearrange("p r o -> p (r o)"),
                                           xt[:, b, k, :], start=(k == 0), stop=(k == KD - 1))
                    mm.then_inc(mm_done[b], 1)
                if some(i):
                    pe.wait_ge(v_out[b], i)
                for k in range(KD):
                    mm = pe.matmul(pv[:, b, 0:D], xt[:, b, k, :], wqkv[:, k, 2 * D:3 * D],
                                   start=(k == 0), stop=(k == KD - 1))
                mm.then_inc(v_mm[b], 1)

            turn(0, 0)
            def pair(i):
                turn(i, 1)
                product(i, 0)
                turn(i + 1, 0)
                product(i, 1)
            pair(0)
            with pe.Fori(1, NPAIR - 1) as i:
                pair(i)
            turn(NPAIR - 1, 1)
            product(NPAIR - 1, 0)
            product(NPAIR - 1, 1)


CHUNKS = [(c, min(1024, N - c)) for c in range(0, N, 1024)]
NC = len(CHUNKS)
TB = 3


def layer1_attention(nc, io, keep, layer1):
    V, ident = keep["V"], keep["ident"]
    QT, KH, KL, adj, adj_in = (layer1[n] for n in ("QT", "KH", "KL", "ADJ1", "adj_in"))
    with Phase(nc, "a1") as ph:
        off = ph.sb("off", [P, N])
        gb = ph.sb("gb", [P, 1])
        sc = ph.sb("sc", [P, H, N])
        wt = ph.sb("wt", [P, NT, P])
        mx = ph.sb("mx", [P, H, NC + 1])
        den = ph.sb("den", [P, 2, H])
        res = ph.sb("res", [P, 2, H, HD])
        qk = ph.ps("qk", [P, 2, 1024])
        tp = ph.ps("tp", [P, TB, 512])
        po = ph.ps("po", [P, 512])
        off_done, scaled_adj, bias_done, r_ok, n_ok, stored, qk_done = (
            ph.sems(f"{n}0 {n}1") for n in
            "off_done scaled_adj bias_done r_ok n_ok stored qk_done".split())
        neg_max, exp_done = (ph.sems(" ".join(f"{n}{h}" for h in range(H))) for n in ("neg_max", "exp_done"))
        masked = [ph.sems(" ".join(f"masked{h}{c}" for c in range(NC))) for h in range(H)]
        turned = ph.sems(" ".join(f"turned{g}" for g in range(NG)))
        copied = ph.sems(" ".join(f"copied{g}" for g in range(NG)))
        heads_in, gb_in = ph.sems("heads_in gb_in")
        block = ph.block()
        by_dve = (1, 4)
        by_act = (0, 2, 3, 5)

        def units(unit):
            i, b, h = unit
            return i * (2 * H) + (b * H + h + 1)

        def tiles(unit):
            i, b, h = unit
            return i * 2 + (b + 1)

        def copies(eng, copy, unit, groups):
            for g in groups:
                n = min(GRP, NT - GRP * g)
                eng.wait_ge(turned[g], units(unit))
                copy(wt[:, GRP * g:GRP * g + n, :], tp[:, g % TB, 0:n * P]).then_inc(copied[g], 1)

        @block.sync
        def _(sp):
            sp.dma_start(gb[:, :], io["L1_gnn_graph_bias"].rearrange("a b c -> (a b) c").to_broadcast([P, 1])
                         ).then_inc(gb_in, 16)

            def store(i, b):
                sp.wait_ge(n_ok[b], i + 1)
                sp.dma_start(keep["OD"][bass.ds((i * 2 + b) * P, P), :],
                             res[:, b, :, :].rearrange("p h o -> p (h o)")).then_inc(stored[b], 16)

            def load(i, b, row):
                sp.wait_ge(masked[H - 1][NC - 1], i * 2 + (b - 1))
                sp.dma_start(adj[:, b, :], io["adj"][bass.ds(row, P), :]).then_inc(adj_in[b], 16)
            with sp.Fori(0, NPAIR - 2) as i:
                for b in range(2):
                    load(i + 1, b, (i * 2 + b + 2) * P)
                    store(i, b)
            load(NPAIR - 1, 0, (NT - 2) * P)
            store(NPAIR - 2, 0)
            load(NPAIR - 1, 1, LAST)
            store(NPAIR - 2, 1)
            for b in range(2):
                store(NPAIR - 1, b)
            for b in range(2):
                sp.wait_ge(stored[b], NPAIR * 16)

        @block.gpsimd
        def _(pool):
            with pool.Fori(0, NPAIR) as i:
                for b in range(2):
                    pool.wait_ge(scaled_adj[b], i + 1)
                    pool.wait_ge(off_done[b], i + 1)
                    pool.nop(nofuse=True)
                    pool.tensor_tensor(adj[:, b, :], adj[:, b, :], off[:, :], ALU.add).then_inc(bias_done[b], 1)

        @block.scalar
        def _(act):
            def exp_part(unit):
                h = unit[2]
                act.wait_ge(neg_max[h], tiles(unit))
                act.activation(sc[:, h, :], sc[:, h, :], ACT.Exp, bias=mx[:, h, NC:NC + 1]
                               ).then_inc(exp_done[h], 1)

            def step(unit):
                copies(act, act.copy, unit, by_act)
                if later(unit, 1):
                    exp_part(later(unit, 1))
            exp_part((0, 0, 0))
            over_units(act, step)

        @block.vector
        def _(dve):
            def scores(unit, chunks):
                i, b, h = unit
                if h == 0 and chunks[0] == 0:
                    dve.wait_ge(bias_done[b], i + 1)
                for c in chunks:
                    c0, cn = CHUNKS[c]
                    s = (h * NC + c) % 2
                    dve.wait_ge(qk_done[s], i * (4 * NC) + (b * 2 * NC + (h * NC + c) // 2 + 1))
                    dve.nop(nofuse=True)
                    dve.tensor_tensor_reduce(sc[:, h, c0:c0 + cn], qk[:, s, 0:cn], adj[:, b, c0:c0 + cn], 1.0,
                                             -BIG, ALU.add, ALU.max, mx[:, h, c:c + 1]).then_inc(masked[h][c], 1)
                if chunks[-1] == NC - 1:
                    for c in range(NC):
                        dve.wait_ge(masked[h][c], tiles(unit))
                    dve.tensor_reduce(mx[:, h, NC:NC + 1], mx[:, h, 0:NC], AX.X, ALU.max,
                                      negate=True).then_inc(neg_max[h], 1)

            def bias(i, b):
                dve.wait_ge(adj_in[b], i * 16 + 16)
                if b:
                    dve.wait_ge(bias_done[0], i + 1)
                elif some(i):
                    dve.wait_ge(bias_done[1], i)
                dve.tensor_scalar(off[:, :], adj[:, b, :], 0.0, MASKED, ALU.is_equal,
                                  ALU.mult).then_inc(off_done[b], 1)
                dve.wait_ge(off_done[b], i + 1)
                dve.tensor_scalar(adj[:, b, :], adj[:, b, :], gb[:, :], None, ALU.mult).then_inc(scaled_adj[b], 1)

            def finish(i, b):
                sums = po[:, 0:H * VW].rearrange("p (h v) -> p h v", h=H)
                dve.wait_ge(heads_in, i * 2 + (b + 1))
                if some(i):
                    dve.wait_ge(stored[b], i * 16)
                dve.reciprocal(den[:, b, :], sums[:, :, HD]).then_inc(r_ok[b], 1)
                dve.wait_ge(r_ok[b], i + 1)
                dve.tensor_tensor(res[:, b, :, :], sums[:, :, 0:HD],
                                  den[:, b, :].rearrange("p (h a) -> p h a", a=1).to_broadcast([P, H, HD]),
                                  ALU.mult).then_inc(n_ok[b], 1)

            def step(unit):
                ahead = later(unit, 2)
                copies(dve, dve.tensor_copy, unit, by_dve[:1])
                if unit[2] == 0 and later(unit, -H):
                    finish(*later(unit, -H)[:2])
                if ahead:
                    scores(ahead, (0,))
                copies(dve, dve.tensor_copy, unit, by_dve[1:])
                if ahead:
                    scores(ahead, (1, 2))
                if unit[2] == 0 and later(unit, H):
                    bias(*later(unit, H)[:2])
            dve.wait_ge(gb_in, 16)
            bias(0, 0)
            scores((0, 0, 0), range(NC))
            scores((0, 0, 1), range(NC))
            over_units(dve, step)
            finish(NPAIR - 1, 1)

        @block.tensor
        def _(pe):
            def products(unit, chunks):
                i, b, h = unit
                for c in chunks:
                    c0, cn = CHUNKS[c]
                    s = (h * NC + c) % 2
                    maximum, number = chunk_read(i, b, h * NC + c - 2)
                    if some(number):
                        pe.wait_ge(maximum, number)
                    for n0 in range(c0, c0 + cn, 512):
                        nn = min(512, c0 + cn - n0)
                        out = qk[:, s, n0 - c0:n0 - c0 + nn]
                        query = QT[:, h, bass.ds((i * 2 + b) * P, P)]
                        pe.matmul(out, query, KH[:, h, n0:n0 + nn], start=True, stop=False)
                        mm = pe.matmul(out, query, KL[:, h, n0:n0 + nn], start=False, stop=True)
                    mm.then_inc(qk_done[s], 1)

            def chunk_read(i, b, k):
                h, c = divmod(k, NC)
                return masked[h % H][c], i * 2 + (b + 1 + h // H)

            def step(unit):
                i, b, h = unit
                ahead = later(unit, 2)
                pe.wait_ge(exp_done[h], tiles(unit))
                for g in range(NG):
                    if g == TB and ahead:
                        products(ahead, (0,))
                    if g >= TB:
                        pe.wait_ge(copied[g - TB], units(unit))
                    for j in range(GRP * g, min(GRP * g + GRP, NT)):
                        col = min(j * P, LAST)
                        mm = pe.transpose(tp[:, g % TB, (j % GRP) * P:(j % GRP + 1) * P],
                                          sc[:, h, col:col + P], ident[:, :])
                    mm.then_inc(turned[g], 1)
                if ahead:
                    products(ahead, (1,))
                if h == 0 and later(unit, -H):
                    before = later(unit, -H)
                    pe.wait_ge(n_ok[before[1]], before[0] + 1)
                for g in range(NG):
                    if g == 2 and ahead:
                        products(ahead, (2,))
                    pe.wait_ge(copied[g], units(unit))
                    for j in range(GRP * g, min(GRP * g + GRP, NT)):
                        mm = pe.matmul(po[:, h * VW:(h + 1) * VW], wt[:, j, :], V[:, j, h, :],
                                       start=(j == 0), stop=(j == NT - 1))
                if h == H - 1:
                    mm.then_inc(heads_in, 1)
            products((0, 0, 0), range(NC))
            products((0, 0, 1), range(NC))
            over_units(pe, step)


def moe_route(nc, io, keep, moe):
    X, ident, neg_half = (keep[n] for n in ("X", "ident", "neg_half"))
    XF, POSI, GW, GD, TE = (moe[n] for n in ("XF", "POSI", "GW", "GD", "TE"))
    NA = TOPK * NT
    with Phase(nc, "m0") as ph:
        gw = ph.sb("gw", [P, KD, E])
        gb = ph.sb("gb", [P, E])
        ones = ph.sb("ones", [P, P])
        before = ph.sb("before", [P, P])
        ie = ph.sb("ie", [P, E])
        steps = ph.sb("steps", [P, NT])
        tiles_i = ph.sb("tiles_i", [1, XTILES])
        st = ph.sb("st", [P, NT, 6])
        mom = ph.sb("mom", [P, 5, NT])
        rs = ph.sb("rs", [P, 4, NT])
        xt = ph.sb("xt", [P, 2, KD, P])
        lg = ph.sb("lg", [P, 2, NT, E])
        eq = ph.sb("eq", [P, NT, E])
        cand = ph.sb("cand", [P, NT, E])
        top = ph.sb("top", [P, 2, NT])
        idx = ph.sb("idx", [P, 2, NT])
        idxp = ph.sb("idxp", [P, 2, NT])
        pick = ph.sb("pick", [P, TOPK, NT, E])
        gap = ph.sb("gap", [P, 4, NT])
        tot = ph.sb("tot", [P, 3, NA, E])
        rank = ph.sb("rank", [P, NA, E])
        cnt = ph.sb("cnt", [P, E, NT])
        til = ph.sb("til", [P, 6, E])
        posf = ph.sb("posf", [P, NA])
        tef = ph.sb("tef", [1, 2, XTILES])
        pt = ph.ps("pt", [P, 2, 512])
        pg = ph.ps("pg", [P, 2, 512])
        pr = ph.ps("pr", [P, 2, 512])
        pc = ph.ps("pc", [P, 2, 512])
        (w_in, ones_ok, consts, stats, moments, inv, pchain, folded, chain, exp_in, exp_ok, picked, ranks,
         scattered, pos_ok, xf_done) = ph.sems(
            "w_in ones_ok consts stats moments inv pchain folded chain exp_in exp_ok picked ranks "
            "scattered pos_ok xf_done")
        turned, xt_done, g_mm, lg_done = (
            ph.sems(f"{n}0 {n}1") for n in "turned xt_done g_mm lg_done".split())
        block = ph.block()

        @block.sync
        def _(sp):
            sp.dma_start(gw[:, :, :], io["L0_ffn_gate_w"].rearrange("(k p) e -> p k e", p=P)).then_inc(w_in, 16)
            sp.dma_start(gb[:, :], bcast_rows(io["L0_ffn_gate_b"], P)).then_inc(w_in, 16)
            for e in range(E):
                sp.dma_start(moe["W1"][:, e, :, :], io["L0_ffn_w1"][e, :, :].rearrange("(k p) f -> p k f", p=P)
                             ).then_inc(moe["w_in"], 16)
                sp.dma_start(moe["W2"][:, e, :, :], io["L0_ffn_w2"][e, :, :].rearrange("(k p) f -> p k f", p=P)
                             ).then_inc(moe["w_in"], 16)

        @block.gpsimd
        def _(pool):
            pool.memset(ones[:, :], 1.0).then_inc(ones_ok, 1)
            pool.memset(before[:, :], 1.0).then_inc(ones_ok, 1)
            pool.wait_ge(ones_ok, 2)
            pool.affine_select(out=before[:, :], in_=before[:, :], compare_op=ALU.is_gt, fill=0.0, base=0,
                               pattern=[[1, P]], channel_multiplier=-1).then_inc(consts, 1)
            for tile, n, step in ((ie, E, 1), (steps, NT, P), (tiles_i, XTILES, 1)):
                pool.iota(tile[:, :], [[step, n]], base=0, channel_multiplier=0,
                          allow_small_or_imprecise_dtypes=True).then_inc(consts, 1)
            for t in range(NT):
                slot_deviation(pool, t, mom, rs, neg_half, moments, pchain, inv)
                standard_rows(pool, XF[:, t:t + 1, :], X[:, t:t + 1, :], rs, t).then_inc(xf_done, 1)
            pool.wait_ge(xf_done, NT)
            pool.wait_ge(pos_ok, 1)
            for j in range(NA):
                pool.indirect_dma_start(keep["XD"], bass.IndirectOffsetOnAxis(POSI[:, j:j + 1], 0),
                                        XF[:, j % NT, :], None).then_inc(scattered, 16)
            pool.wait_ge(scattered, 16 * NA)

        @block.tensor
        def _(pe):
            pe.wait_ge(w_in, 32)

            def turn(i, b):
                t = i * 2 + b
                pe.wait_ge(xf_done, t + 1)
                if some(i):
                    pe.wait_ge(xt_done[b], i)
                for k in range(KD):
                    mm = pe.transpose(pt[:, b, k * P:(k + 1) * P], XF[:, t, k * P:(k + 1) * P], ident[:, :])
                mm.then_inc(turned[b], 1)

            def product(i, b):
                pe.wait_ge(xt_done[b], i + 1)
                if some(i):
                    pe.wait_ge(lg_done[b], i)
                for k in range(KD):
                    mm = pe.matmul(pg[:, b, 0:E], xt[:, b, k, :], gw[:, k, :], start=(k == 0), stop=(k == KD - 1))
                mm.then_inc(g_mm[b], 1)
            turn(0, 0)
            for i in range(NPAIR):
                turn(i, 1)
                product(i, 0)
                if i < NPAIR - 1:
                    turn(i + 1, 0)
                product(i, 1)
            pe.wait_ge(consts, 1)
            pe.wait_ge(ones_ok, 1)
            pe.wait_ge(picked, 2)
            for k in range(TOPK):
                pe.matmul(pr[:, k, 0:NT * E], before[:, :], pick[:, k, :, :].rearrange("p t e -> p (t e)"),
                          start=True, stop=True)
                mm = pe.matmul(pc[:, k, 0:NT * E], ones[:, :], pick[:, k, :, :].rearrange("p t e -> p (t e)"),
                               start=True, stop=True)
            mm.then_inc(ranks, 1)

        @block.scalar
        def _(act):
            with act.Fori(0, NPAIR) as i:
                for b in range(2):
                    act.wait_ge(turned[b], i + 1)
                    act.copy(xt[:, b, :, :], pt[:, b, 0:D]).then_inc(xt_done[b], 1)
            act.wait_ge(exp_in, 1)
            act.activation(gap[:, 1, :], gap[:, 0, :], ACT.Exp).then_inc(exp_ok, 1)

        @block.vector
        def _(dve):
            slot_moments(dve, X, st, mom, stats, folded, moments)
            dve.wait_ge(w_in, 32)
            with dve.Fori(0, NPAIR) as i:
                for b in range(2):
                    dve.wait_ge(g_mm[b], i + 1)
                    dve.tensor_tensor(lg[:, 0, bass.ds(i * 2 + b, 1), :], pg[:, b:b + 1, 0:E],
                                      gb[:, :].rearrange("p (a e) -> p a e", a=1), ALU.add).then_inc(lg_done[b], 1)
            for b in range(2):
                dve.wait_ge(lg_done[b], NPAIR)
            dve.wait_ge(consts, 4)
            n = [0]

            def link(ins):
                n[0] += 1
                ins.then_inc(chain, 1)
                dve.wait_ge(chain, n[0])

            def over_experts(ap):
                return ap.rearrange("p (t a) -> p t a", a=1).to_broadcast([P, NT, E])
            ie_all = ie[:, :].rearrange("p (a e) -> p a e", a=1).to_broadcast([P, NT, E])
            for k in range(TOPK):
                link(dve.tensor_reduce(top[:, k, :], lg[:, k, :, :], AX.X, ALU.max))
                link(dve.tensor_tensor(eq[:, :, :], lg[:, k, :, :], over_experts(top[:, k, :]), ALU.is_equal))
                link(dve.scalar_tensor_tensor(cand[:, :, :], eq[:, :, :], -float(E), ie_all, ALU.mult, ALU.add))
                link(dve.tensor_reduce(idx[:, k, :], cand[:, :, :], AX.X, ALU.min))
                link(dve.tensor_scalar(idxp[:, k, :], idx[:, k, :], float(E), None, ALU.add))
                dve.tensor_tensor(pick[:, k, :, :], over_experts(idxp[:, k, :]), ie_all,
                                  ALU.is_equal).then_inc(picked, 1)
                dve.wait_ge(picked, k + 1)
                if k == 0:
                    link(dve.scalar_tensor_tensor(lg[:, 1, :, :], pick[:, 0, :, :], -BIG, lg[:, 0, :, :],
                                                  ALU.mult, ALU.add))
            dve.tensor_tensor(gap[:, 0, :], top[:, 1, :], top[:, 0, :], ALU.subtract).then_inc(exp_in, 1)

            dve.wait_ge(ranks, 1)
            for k in range(TOPK):
                cols = slice(k * NT, (k + 1) * NT)
                dve.tensor_copy(rank[:, cols, :], pr[:, k, 0:NT * E])
                dve.tensor_copy(tot[:, 0, cols, :], pc[:, k, 0:NT * E])
                link(dve.tensor_copy(tot[:, 1, cols, :], pc[:, k, 0:NT * E]))
            src, s = 1, 1
            while s < NA:
                dst = 3 - src
                dve.tensor_copy(tot[:, dst, 0:s, :], tot[:, src, 0:s, :])
                link(dve.tensor_tensor(tot[:, dst, s:NA, :], tot[:, src, s:NA, :], tot[:, src, 0:NA - s, :], ALU.add))
                src, s = dst, 2 * s
            count = tot[:, src, NA - 1, :]
            link(dve.tensor_tensor(cnt[:, :, :], count.rearrange("p (e a) -> p e a", a=1).to_broadcast([P, E, NT]),
                                   steps[:, :].rearrange("p (a t) -> p a t", a=1).to_broadcast([P, E, NT]),
                                   ALU.is_gt))
            dve.tensor_reduce(til[:, 0, :], cnt[:, :, :], AX.X, ALU.add)
            link(dve.tensor_reduce(til[:, 1, :], cnt[:, :, :], AX.X, ALU.add))
            tsrc, s = 1, 1
            while s < E:
                dst = 3 - tsrc
                dve.tensor_copy(til[:, dst, 0:s], til[:, tsrc, 0:s])
                link(dve.tensor_tensor(til[:, dst, s:E], til[:, tsrc, s:E], til[:, tsrc, 0:E - s], ALU.add))
                tsrc, s = dst, 2 * s
            ends = til[:, tsrc, :]
            link(dve.tensor_tensor(til[:, 3, :], ends, til[:, 0, :], ALU.subtract))
            link(dve.tensor_scalar(til[:, 4, :], til[:, 3, :], float(P), None, ALU.mult))
            here = tot[:, 3 - src, :, :]
            link(dve.tensor_tensor(here, tot[:, src, :, :], tot[:, 0, :, :], ALU.subtract))
            link(dve.tensor_tensor(rank[:, :, :], here, rank[:, :, :], ALU.add))
            link(dve.tensor_tensor(rank[:, :, :], rank[:, :, :],
                                   til[:, 4, :].rearrange("p (a e) -> p a e", a=1).to_broadcast([P, NA, E]), ALU.add))
            link(dve.tensor_tensor(rank[:, :, :], rank[:, :, :], pick[:, :, :, :].rearrange("p k t e -> p (k t) e"),
                                   ALU.mult))
            link(dve.tensor_reduce(posf[:, :], rank[:, :, :], AX.X, ALU.add))
            dve.tensor_copy(POSI[:, :], posf[:, :]).then_inc(pos_ok, 1)
            dve.wait_ge(exp_ok, 1)
            link(dve.tensor_scalar(gap[:, 2, :], gap[:, 1, :], 1.0, None, ALU.add))
            link(dve.reciprocal(GW[:, 0, :], gap[:, 2, :]))
            link(dve.tensor_tensor(GW[:, 1, :], gap[:, 1, :], GW[:, 0, :], ALU.mult))
            for k in range(TOPK):
                share = (eq, cand)[k]
                link(dve.tensor_tensor(share[:, :, :], pick[:, k, :, :], over_experts(GW[:, k, :]), ALU.mult))
            link(dve.tensor_tensor(GD[:, :, :], eq[:, :, :], cand[:, :, :], ALU.add))
            tcmp = tot[0:1, :, :, :].rearrange("p j a e -> p (j a) e")[:, 0:XTILES, :]
            link(dve.tensor_tensor(tcmp, ends[0:1, :].rearrange("p (a e) -> p a e", a=1).to_broadcast([1, XTILES, E]),
                                   tiles_i[:, :].rearrange("p (t a) -> p t a", a=1).to_broadcast([1, XTILES, E]),
                                   ALU.is_le))
            link(dve.tensor_reduce(tef[:, 0, :], tcmp, AX.X, ALU.add))
            link(dve.tensor_scalar(tef[:, 1, :], tef[:, 0, :], float(E - 1), None, ALU.min))
            link(dve.tensor_copy(TE[:, :], tef[:, 1, :]))


def moe_experts(nc, io, keep, moe):
    ident, TE, W1, W2, w_in = keep["ident"], moe["TE"], moe["W1"], moe["W2"], moe["w_in"]
    PAIRS = XTILES // 2
    with Phase(nc, "m1") as ph:
        w1 = ph.sb("w1", [P, 2, KD, F])
        b1 = ph.sb("b1", [P, E * FB])
        b1n = ph.sb("b1n", [E * FB, P])
        rows = ph.sb("rows", [P, 2, D])
        xt = ph.sb("xt", [P, 2, KD, P])
        hid = ph.sb("hid", [P, 2, FB, P])
        y = ph.sb("y", [P, 2, D])
        pt = ph.ps("pt", [P, 2, 512])
        p1 = ph.ps("p1", [P, 2, 512])
        p2 = ph.ps("p2", [P, 2, 512])
        pb = ph.ps("pb", [P, 512])
        b_in, b_ps, b_ok = ph.sems("b_in b_ps b_ok")
        staged, rows_in, turned, xt_done, hid_mm, hid_done, y_mm, y_done, stored = (
            ph.sems(f"{n}0 {n}1") for n in
            "staged rows_in turned xt_done hid_mm hid_done y_mm y_done stored".split())
        block = ph.block()

        def expert_of(eng, i, b):
            return eng.value_load(TE[0:1, bass.ds(i * 2 + b, 1)], min_val=0, max_val=E - 1)

        @block.sync
        def _(sp):
            sp.dma_start(b1n[:, :], io["L0_ffn_b1"].rearrange("e (f p) -> (e f) p", p=P)).then_inc(b_in, 16)

            def load(i, b):
                if some(i):
                    sp.wait_ge(turned[b], i)
                sp.dma_start(rows[:, b, :], keep["XD"][bass.ds((i * 2 + b) * P, P), :]).then_inc(rows_in[b], 16)
            for b in range(2):
                load(0, b)
            with sp.Fori(1, PAIRS) as i:
                for b in range(2):
                    load(i, b)

        @block.tensor
        def _(pe):
            pe.wait_ge(b_in, 16)
            pe.transpose(pb[:, 0:E * FB], b1n[:, :], ident[0:E * FB, 0:E * FB]).then_inc(b_ps, 1)

            def turn(i, b):
                pe.wait_ge(rows_in[b], i * 16 + 16)
                if some(i):
                    pe.wait_ge(xt_done[b], i)
                for k in range(KD):
                    mm = pe.transpose(pt[:, b, k * P:(k + 1) * P], rows[:, b, k * P:(k + 1) * P], ident[:, :])
                mm.then_inc(turned[b], 1)

            def up(i, b):
                pe.wait_ge(staged[b], i + 1)
                pe.wait_ge(xt_done[b], i + 1)
                if some(i):
                    pe.wait_ge(hid_done[b], i * FB)
                for f in range(FB):
                    for k in range(KD):
                        mm = pe.matmul(p1[:, b, f * P:(f + 1) * P], w1[:, b, k, f * P:(f + 1) * P], xt[:, b, k, :],
                                       start=(k == 0), stop=(k == KD - 1))
                mm.then_inc(hid_mm[b], 1)

            def down(i, b):
                e = expert_of(pe, i, b)
                pe.wait_ge(hid_done[b], i * FB + FB)
                if some(i):
                    pe.wait_ge(y_done[b], i)
                for f in range(FB):
                    mm = pe.matmul(p2[:, b, 0:D], hid[:, b, f, :], W2[:, bass.ds(e, 1), f, :],
                                   start=(f == 0), stop=(f == FB - 1))
                mm.then_inc(y_mm[b], 1)

            turn(0, 0)
            turn(0, 1)
            up(0, 0)

            def pair(i):
                up(i, 1)
                turn(i + 1, 0)
                down(i, 0)
                up(i + 1, 0)
                turn(i + 1, 1)
                down(i, 1)
            pair(0)
            with pe.Fori(1, PAIRS - 1) as i:
                pair(i)
            up(PAIRS - 1, 1)
            down(PAIRS - 1, 0)
            down(PAIRS - 1, 1)

        @block.vector
        def _(dve):
            dve.wait_ge(w_in, 2 * 16 * E)

            def stage(i, b):
                e = expert_of(dve, i, b)
                if some(i):
                    dve.wait_ge(hid_mm[b], i)
                dve.tensor_copy(w1[:, b:b + 1, :, :], W1[:, bass.ds(e, 1), :, :]).then_inc(staged[b], 1)
                dve.wait_ge(turned[b], i + 1)
                dve.tensor_copy(xt[:, b, :, :], pt[:, b, 0:D]).then_inc(xt_done[b], 1)

            def y_out(i, b):
                dve.wait_ge(y_mm[b], i + 1)
                if some(i):
                    dve.wait_ge(stored[b], i * 16)
                dve.tensor_copy(y[:, b, :], p2[:, b, 0:D]).then_inc(y_done[b], 1)
            stage(0, 0)
            stage(0, 1)

            def pair(i):
                stage(i + 1, 0)
                y_out(i, 0)
                stage(i + 1, 1)
                y_out(i, 1)
            pair(0)
            with dve.Fori(1, PAIRS - 1) as i:
                pair(i)
            y_out(PAIRS - 1, 0)
            y_out(PAIRS - 1, 1)

        @block.scalar
        def _(act):
            act.wait_ge(b_ps, 1)
            act.copy(b1[:, :], pb[:, 0:E * FB]).then_inc(b_ok, 1)
            act.wait_ge(b_ok, 1)
            with act.Fori(0, PAIRS) as i:
                for b in range(2):
                    e = expert_of(act, i, b)
                    act.wait_ge(hid_mm[b], i + 1)
                    for f in range(FB):
                        act.activation(hid[:, b, f, :], p1[:, b, f * P:(f + 1) * P], ACT.Relu,
                                       bias=b1[:, bass.ds(e * FB + f, 1)]).then_inc(hid_done[b], 1)

        @block.gpsimd
        def _(pool):
            with pool.Fori(0, PAIRS) as i:
                for b in range(2):
                    pool.wait_ge(y_done[b], i + 1)
                    pool.dma_start(keep["YD"][bass.ds((i * 2 + b) * P, P), :], y[:, b, :]).then_inc(stored[b], 16)
            for b in range(2):
                pool.wait_ge(stored[b], PAIRS * 16)


def moe_combine(nc, io, keep, moe):
    X, ident, neg_half = (keep[n] for n in ("X", "ident", "neg_half"))
    XF, POSI, GW, GD = (moe[n] for n in ("XF", "POSI", "GW", "GD"))
    NA = TOPK * NT
    with Phase(nc, "m2") as ph:
        b2 = ph.sb("b2", [E, D])
        affine = ph.sb("affine", [P, 2, D])
        got = ph.sb("got", [P, NA, D])
        st = ph.sb("st", [P, NT, 6])
        mom = ph.sb("mom", [P, 5, NT])
        rs = ph.sb("rs", [P, 4, NT])
        z = ph.sb("z", [P, 2, D])
        zz = ph.sb("zz", [P, 2, D])
        gt = ph.sb("gt", [E, 2, P])
        pb = ph.ps("pb", [P, 2, 512])
        pt = ph.ps("pt", [P, 2, 512])
        w_in, stats, folded, moments, pchain, inv, biased = ph.sems(
            "w_in stats folded moments pchain inv biased")
        gathered = ph.sems(" ".join(f"gathered{k}" for k in range(len(BATCHES))))
        gt_ps, gt_sb, b_mm, first, second, third, z_done, zz_done, x_out = (
            ph.sems(f"{n}0 {n}1") for n in
            "gt_ps gt_sb b_mm first second third z_done zz_done x_out".split())
        block = ph.block()

        @block.sync
        def _(sp):
            sp.dma_start(b2[:, :], io["L0_ffn_b2"]).then_inc(w_in, 16)
            for j, name in enumerate(("L0_ffn_gamma", "L0_ffn_beta")):
                sp.dma_start(affine[:, j, :], bcast_rows(io[name], P)).then_inc(w_in, 16)

        @block.gpsimd
        def _(pool):
            for k, (a, end) in enumerate(BATCHES):
                for t in range(2 * a, 2 * end):
                    for j in (t, NT + t):
                        pool.indirect_dma_start(got[:, j, :], None, keep["YD"],
                                                bass.IndirectOffsetOnAxis(POSI[:, j:j + 1], 0)
                                                ).then_inc(gathered[k], 16)
            pool.wait_ge(w_in, 48)
            with pool.Fori(0, NT) as t:
                xs = X[:, bass.ds(t, 1), :]
                pool.tensor_tensor(xs, xs, affine[:, 1:2, :], ALU.add).then_inc(biased, 1)
            pool.wait_ge(moments, 1)
            inverse_deviation(pool, mom, rs, neg_half, 0, NT, pchain, 0).then_inc(inv, 1)
            pool.wait_ge(biased, NT)
            for t in range(NT):
                pool.wait_ge(zz_done[t % 2], t // 2 + 1)
                pool.tensor_tensor(X[:, t:t + 1, :], X[:, t:t + 1, :], zz[:, t % 2:t % 2 + 1, :],
                                   ALU.add).then_inc(x_out[t % 2], 1)

        @block.tensor
        def _(pe):
            pe.wait_ge(w_in, 48)
            for t in range(NT):
                i, b = divmod(t, 2)
                if some(i):
                    pe.wait_ge(gt_sb[b], i)
                pe.transpose(pt[0:E, b, 0:P], GD[:, t, :], ident[:, :]).then_inc(gt_ps[b], 1)
                pe.wait_ge(gt_sb[b], i + 1)
                if some(i):
                    pe.wait_ge(third[b], i)
                pe.matmul(pb[:, b, 0:D], gt[:, b, :], b2[:, :], start=True, stop=True).then_inc(b_mm[b], 1)

        @block.scalar
        def _(act):
            for t in range(NT):
                i, b = divmod(t, 2)
                act.wait_ge(gt_ps[b], i + 1)
                if some(i):
                    act.wait_ge(b_mm[b], i)
                act.copy(gt[:, b, :], pt[0:E, b, 0:P]).then_inc(gt_sb[b], 1)
            act.wait_ge(inv, 1)
            for t in range(NT):
                i, b = divmod(t, 2)
                if some(i):
                    act.wait_ge(zz_done[b], i)
                act.activation(z[:, b, :], XF[:, t, :], ACT.Identity, scale=rs[:, 0, t:t + 1],
                               bias=rs[:, 1, t:t + 1]).then_inc(z_done[b], 1)

        @block.vector
        def _(dve):
            def weigh(i):
                rows = [XF[:, bass.ds(i * 2 + b, 1), :] for b in range(2)]
                for k, done in enumerate((first, second)):
                    for b in range(2):
                        t = i * 2 + b
                        if k:
                            dve.wait_ge(first[b], i + 1)
                        dve.scalar_tensor_tensor(rows[b], got[:, bass.ds(t + k * NT, 1), :],
                                                 GW[:, k, bass.ds(t, 1)], rows[b], ALU.mult,
                                                 ALU.add).then_inc(done[b], 1)
                for b in range(2):
                    dve.wait_ge(second[b], i + 1)
                    dve.wait_ge(b_mm[b], i + 1)
                    dve.tensor_tensor(rows[b], pb[:, b:b + 1, 0:D], rows[b], ALU.add).then_inc(third[b], 1)
                for b in range(2):
                    dve.wait_ge(third[b], i + 1)
                    dve.bn_stats(st[:, bass.ds(i * 2 + b, 1), :], rows[b]).then_inc(stats, 1)
            for k, (a, end) in enumerate(BATCHES):
                dve.wait_ge(gathered[k], 16 * TOPK * 2 * (end - a))
                with dve.Fori(a, end) as i:
                    weigh(i)
            dve.wait_ge(stats, NT)
            row_moments(dve, st, mom, 0, NT, folded, 0).then_inc(moments, 1)
            dve.wait_ge(w_in, 48)
            for t in range(NT):
                i, b = divmod(t, 2)
                dve.wait_ge(z_done[b], i + 1)
                if some(i):
                    dve.wait_ge(x_out[b], i)
                dve.tensor_tensor(zz[:, b, :], z[:, b, :], affine[:, 0, :], ALU.mult).then_inc(zz_done[b], 1)


def layer1_project(nc, io, keep):
    X, ident = keep["X"], keep["ident"]
    with Phase(nc, "o1") as ph:
        wout = ph.sb("wout", [P, KD, D])
        bout = ph.sb("bout", [P, D])
        o = ph.sb("o", [P, NT, D])
        ot = ph.sb("ot", [P, 2, KD, P])
        pt = ph.ps("pt", [P, 2, 512])
        py = ph.ps("py", [P, 2, 512])
        (w_in,) = ph.sems("w_in")
        o_in = ph.sems(" ".join(f"o_in{k}" for k in range(len(BATCHES))))
        turned, ot_done, y_mm, biased, x_out = (
            ph.sems(f"{n}0 {n}1") for n in "turned ot_done y_mm biased x_out".split())
        block = ph.block()

        @block.sync
        def _(sp):
            for k, (a, end) in enumerate(BATCHES):
                s0, s1 = 2 * a, 2 * end
                sp.dma_start(o[:, s0:s1, :], keep["OD"][P * s0:P * s1, :].rearrange("(t p) d -> p t d", p=P)
                             ).then_inc(o_in[k], 16)
            sp.dma_start(wout[:, :, :], io["L1_gnn_Wout"].rearrange("(k p) o -> p k o", p=P)).then_inc(w_in, 16)
            sp.dma_start(bout[:, :], bcast_rows(io["L1_gnn_bout"], P)).then_inc(w_in, 16)

        @block.gpsimd
        def _(pool):
            pool.wait_ge(w_in, 32)
            with pool.Fori(0, NPAIR) as i:
                for b in range(2):
                    xs = X[:, bass.ds(i * 2 + b, 1), :]
                    pool.tensor_tensor(xs, xs, bout[:, :].rearrange("p (a d) -> p a d", a=1),
                                       ALU.add).then_inc(biased[b], 1)

        @block.scalar
        def _(act):
            with act.Fori(0, NPAIR) as i:
                for b in range(2):
                    act.wait_ge(turned[b], i + 1)
                    act.copy(ot[:, b, :, :], pt[:, b, 0:D]).then_inc(ot_done[b], 1)

        @block.vector
        def _(dve):
            with dve.Fori(0, NPAIR) as i:
                for b in range(2):
                    dve.wait_ge(y_mm[b], i + 1)
                    dve.wait_ge(biased[b], i + 1)
                    xs = X[:, bass.ds(i * 2 + b, 1), :]
                    dve.tensor_tensor(xs, py[:, b:b + 1, 0:D], xs, ALU.add).then_inc(x_out[b], 1)

        @block.tensor
        def _(pe):
            pe.wait_ge(w_in, 32)

            def turn(i, b):
                for k, (a, _) in enumerate(BATCHES):
                    if (i, b) == (a, 0):
                        pe.wait_ge(o_in[k], 16)
                if some(i):
                    pe.wait_ge(ot_done[b], i)
                for k in range(KD):
                    mm = pe.transpose(pt[:, b, k * P:(k + 1) * P], o[:, i * 2 + b, k * P:(k + 1) * P], ident[:, :])
                mm.then_inc(turned[b], 1)

            def product(i, b):
                pe.wait_ge(ot_done[b], i + 1)
                if some(i):
                    pe.wait_ge(x_out[b], i)
                for k in range(KD):
                    mm = pe.matmul(py[:, b, 0:D], ot[:, b, k, :], wout[:, k, :],
                                   start=(k == 0), stop=(k == KD - 1))
                mm.then_inc(y_mm[b], 1)
            turn(0, 0)
            for i in range(NPAIR):
                turn(i, 1)
                product(i, 0)
                if i < NPAIR - 1:
                    turn(i + 1, 0)
                product(i, 1)


RING = 4
LAG = 3


def layer1_ffn(nc, io, keep):
    X, ident, neg_half = (keep[n] for n in ("X", "ident", "neg_half"))
    with Phase(nc, "f1") as ph:
        wn = ph.sb("wn", [P, KD, D])
        wt = ph.sb("wt", [P, KD, KD, P])
        wl = ph.sb("wl", [P, KD, KD * P])
        lnwb = ph.sb("lnwb", [P, 2, KD])
        lb3 = ph.sb("lb3", [P, KD, 3])
        ones = ph.sb("ones", [P, P])
        b3 = ph.sb("b3", [3, D])
        c3 = ph.sb("c3", [3, 3, D])
        parts = ph.sb("parts", [3, 3, D], BF16)
        sel = ph.sb("sel", [3, 3, D])
        crow = ph.sb("crow", [3, D], BF16)
        ones3 = ph.sb("ones3", [3, P], BF16)
        th = ph.sb("th", [P, NPAIR, 2, D])
        gg = ph.sb("gg", [P, NPAIR, 2, D])
        yt = ph.sb("yt", [P, RING, 2, KD, P])
        st = ph.sb("st", [P, NT, 6])
        mom = ph.sb("mom", [P, 5, NT])
        rs = ph.sb("rs", [P, 4, NT])
        pt = ph.ps("pt", [P, RING, 512])
        pm = ph.ps("pm", [P, RING, 512])
        (w_in, w_ps, w_sb, w_scaled, ones_done, c_mm, cchain, c_done, x_stats, x_folded, x_moments, x_pchain,
         x_inv, h_done, out_done, stored) = ph.sems(
            "w_in w_ps w_sb w_scaled ones_done c_mm cchain c_done x_stats x_folded x_moments x_pchain "
            "x_inv h_done out_done stored")
        each = lambda n: ph.sems(" ".join(f"{n}{g}" for g in range(NPAIR)))
        turned, yt_done, h_mm, tanh_done, g_done, silu_done, stat_done, y_done, res_done = (
            each(n) for n in "turned yt_done h_mm tanh_done g_done silu_done stat_done y_done res_done".split())
        folded, moments, pchain, inv = (ph.sems(" ".join(f"{n}{k}" for k in range(len(BATCHES))))
                                        for n in "folded moments pchain inv".split())
        block = ph.block()

        def last_user(g):
            same = [q for q in range(NPAIR) if q % RING == g % RING]
            at = same.index(g)
            return (same[at - 1], at > 0)

        def batch_of(g):
            return next(k for k, (a, z) in enumerate(BATCHES) if a <= g < z)

        @block.sync
        def _(sp):
            sp.dma_start(wn[:, :, :], io["L1_ffn_W"].rearrange("(k p) o -> p k o", p=P)).then_inc(w_in, 16)
            sp.dma_start(b3[:, :], bcast_rows(io["L1_ffn_b"], 3)).then_inc(w_in, 16)
            with nc.allow_non_contiguous_dma(reason="two columns of 128"):
                for j, name in enumerate(("L1_ffn_ln_w", "L1_ffn_ln_b")):
                    sp.dma_start(lnwb[:, j, :], io[name].rearrange("(k p) -> p k", p=P)).then_inc(w_in, 16)
            for g in range(NPAIR):
                sp.wait_ge(out_done, g + 1)
                for r in range(2):
                    t = 2 * g + r
                    if t < NT - 1:
                        sp.dma_start(io["out"][t * P:(t + 1) * P, :], X[:, t, :]).then_inc(stored, 16)
                    else:
                        sp.dma_start(io["out"][t * P:N, :], X[OVER:P, t, :]).then_inc(stored, 16)
            sp.wait_ge(stored, NT * 16)

        def elementwise_dve(dve, i, src):
            def blend(g):
                dve.wait_ge(tanh_done[g], i + 1)
                dve.scalar_tensor_tensor(gg[:, g, :, :], th[:, g, :, :], 0.01, src(g), ALU.mult,
                                         ALU.add).then_inc(g_done[g], 1)

            def stats(g):
                dve.wait_ge(silu_done[g], i + 1)
                for r in range(2):
                    dve.bn_stats(st[:, 2 * g + r, :], th[:, g, r, :]).then_inc(stat_done[g], 1)
                k = batch_of(g)
                if g == BATCHES[k][1] - 1:
                    a, z = BATCHES[k]
                    for q in range(a, z):
                        dve.wait_ge(stat_done[q], i * 2 + 2)
                    row_moments(dve, st, mom, 2 * a, 2 * z, folded[k], i * 3).then_inc(moments[k], 1)
            for g in range(NPAIR):
                blend(g)
                if g >= 2:
                    stats(g - 2)
            stats(NPAIR - 2)
            stats(NPAIR - 1)

        def elementwise_pool(pool, i):
            for k, (a, z) in enumerate(BATCHES):
                pool.wait_ge(moments[k], i + 1)
                pool.nop(nofuse=True)
                inverse_deviation(pool, mom, rs, neg_half, 2 * a, 2 * z, pchain[k], i * 3).then_inc(inv[k], 1)
                pool.wait_ge(inv[k], i + 1)
                pool.nop(nofuse=True)
                for g in range(a, z):
                    for r in range(2):
                        standard_rows(pool, gg[:, g, r:r + 1, :], th[:, g, r:r + 1, :], rs,
                                      2 * g + r).then_inc(y_done[g], 1)

        @block.gpsimd
        def _(pool):
            pool.memset(ones[:, :], 1.0).then_inc(ones_done, 1)
            pool.memset(ones3[:, :], 1.0).then_inc(ones_done, 1)
            for g in range(NPAIR):
                slot_deviation(pool, 2 * g, mom, rs, neg_half, x_moments, x_pchain, x_inv)
                for r in range(2):
                    standard_rows(pool, gg[:, g, r:r + 1, :], X[:, 2 * g + r:2 * g + r + 1, :], rs,
                                  2 * g + r).then_inc(h_done, 1)
            elementwise_pool(pool, 0)
            with pool.Fori(1, ITERS) as i:
                elementwise_pool(pool, i)

        @block.vector
        def _(dve):
            slot_moments(dve, X, st, mom, x_stats, x_folded, x_moments)
            dve.wait_ge(w_in, 64)
            dve.wait_ge(ones_done, 2)
            for k in range(KD):
                dve.tensor_scalar(lb3[:, k, :], ones[:, 0:3], lnwb[:, 1, k:k + 1], None, ALU.mult).then_inc(w_scaled, 1)
            dve.wait_ge(w_sb, 1)
            for k in range(KD):
                dve.tensor_scalar(wl[:, k, :], wt[:, k, :, :].rearrange("p j o -> p (j o)"),
                                  lnwb[:, 0, k:k + 1], None, ALU.mult).then_inc(w_scaled, 1)
            dve.wait_ge(c_mm, 1)
            dve.tensor_tensor(c3[:, 0, :], pm[0:3, 0, 0:D], b3[:, :], ALU.add).then_inc(cchain, 1)
            n = 1
            for r in range(3):
                dve.wait_ge(cchain, n)
                dve.tensor_copy(parts[:, r, :], c3[:, r, :]).then_inc(cchain, 1)
                n += 1
                dve.wait_ge(cchain, n)
                if r < 2:
                    dve.tensor_tensor(c3[:, r + 1, :], c3[:, r, :], parts[:, r, :], ALU.subtract).then_inc(cchain, 1)
                    n += 1
            dve.tensor_scalar(sel[:, 0, :], parts[:, 0, :], ident[0:3, 0:1], None, ALU.mult).then_inc(cchain, 1)
            dve.wait_ge(cchain, n + 1)
            dve.scalar_tensor_tensor(sel[:, 1, :], parts[:, 1, :], ident[0:3, 1:2], sel[:, 0, :], ALU.mult,
                                     ALU.add).then_inc(cchain, 1)
            dve.wait_ge(cchain, n + 2)
            dve.scalar_tensor_tensor(crow[:, :], parts[:, 2, :], ident[0:3, 2:3], sel[:, 1, :], ALU.mult,
                                     ALU.add).then_inc(c_done, 1)

            elementwise_dve(dve, 0, lambda g: gg[:, g, :, :])
            with dve.Fori(1, ITERS) as i:
                elementwise_dve(dve, i, lambda g: pm[:, g % RING, :].rearrange("p (r d) -> p r d", r=2))
            for g in range(NPAIR):
                dve.wait_ge(h_mm[g], ITERS)
                dve.tensor_tensor(X[:, 2 * g:2 * g + 2, :], pm[:, g % RING, :].rearrange("p (r d) -> p r d", r=2),
                                  X[:, 2 * g:2 * g + 2, :], ALU.add).then_inc(out_done, 1)

        def act_stream(act, i, first):
            def turned_out(g):
                act.wait_ge(turned[g], i)
                act.copy(yt[:, g % RING, :, :, :], pt[:, g % RING, :]).then_inc(yt_done[g], 1)

            def tanh(g):
                if first:
                    act.wait_ge(h_done, 2 * g + 2)
                    src = gg[:, g, :, :]
                else:
                    act.wait_ge(h_mm[g], i)
                    act.wait_ge(y_done[g], i * 2)
                    src = pm[:, g % RING, :]
                act.activation(th[:, g, :, :], src, ACT.Tanh).then_inc(tanh_done[g], 1)

            def silu(g):
                act.wait_ge(g_done[g], i + 1)
                act.activation(th[:, g, :, :], gg[:, g, :, :], ACT.Silu).then_inc(silu_done[g], 1)
            for g in range(NPAIR + LAG + 1):
                if g < NPAIR and not first:
                    turned_out(g)
                if LAG <= g < NPAIR + LAG:
                    tanh(g - LAG)
                if g > LAG:
                    silu(g - LAG - 1)

        @block.scalar
        def _(act):
            act.wait_ge(w_ps, 1)
            act.copy(wt[:, :, :, :], pt[:, 0, :]).then_inc(w_sb, 1)
            act_stream(act, 0, True)
            with act.Fori(1, ITERS) as i:
                act_stream(act, i, False)
            for g in range(NPAIR):
                act.wait_ge(turned[g], ITERS)
                act.copy(yt[:, g % RING, :, :, :], pt[:, g % RING, :]).then_inc(yt_done[g], 1)

        def pe_stream(pe, i, last):
            def turn(g):
                q, here = last_user(g)
                pe.wait_ge(y_done[g], i * 2)
                if here or some(i - 1):
                    pe.wait_ge(yt_done[q], i if here else i - 1)
                for r in range(2):
                    for k in range(KD):
                        mm = pe.transpose(pt[:, g % RING, (r * KD + k) * P:(r * KD + k + 1) * P],
                                          gg[:, g, r, k * P:(k + 1) * P], ident[:, :])
                mm.then_inc(turned[g], 1)

            def product(g):
                q, here = last_user(g)
                pe.wait_ge(yt_done[g], i)
                if here and last:
                    pe.wait_ge(out_done, q + 1)
                elif here:
                    pe.wait_ge(g_done[q], i + 1)
                else:
                    pe.wait_ge(g_done[q], i)
                for r in range(2):
                    out = pm[:, g % RING, r * D:(r + 1) * D]
                    for k in range(KD):
                        pe.matmul(out, yt[:, g % RING, r, k, :], wl[:, k, :], start=(k == 0), stop=False)
                    mm = pe.matmul(out, ones3[:, :], crow[:, :], start=False, stop=True)
                mm.then_inc(h_mm[g], 1)
            for g in range(NPAIR + LAG):
                if g < NPAIR:
                    turn(g)
                if g >= LAG:
                    product(g - LAG)

        @block.tensor
        def _(pe):
            pe.wait_ge(w_in, 64)
            for k in range(KD):
                for j in range(KD):
                    mm = pe.transpose(pt[:, 0, (k * KD + j) * P:(k * KD + j + 1) * P],
                                      wn[:, j, k * P:(k + 1) * P], ident[:, :])
            mm.then_inc(w_ps, 1)
            pe.wait_ge(w_sb, 1)
            pe.wait_ge(w_scaled, KD)
            for k in range(KD):
                mm = pe.matmul(pm[0:3, 0, 0:D], lb3[:, k, :], wt[:, k, :, :].rearrange("p j o -> p (j o)"),
                               start=(k == 0), stop=(k == KD - 1))
            mm.then_inc(c_mm, 1)
            pe.wait_ge(w_scaled, 2 * KD)
            pe.wait_ge(c_done, 1)
            pe_stream(pe, 1, False)
            with pe.Fori(2, ITERS) as i:
                pe_stream(pe, i, False)
            pe_stream(pe, ITERS, True)


def build(nc, io):
    with ExitStack() as whole:
        def buffers(ctx, **shapes):
            return {n: ctx.enter_context(nc.sbuf_tensor(n, s[0], s[1] if len(s) > 1 else F32))
                    for n, s in shapes.items()}

        keep = buffers(whole, X=([P, NT, D],), ident=([P, P],), neg_half=([P, NT],))
        for name, rows in (("XD", XTILES * P), ("YD", XTILES * P), ("OD", NT * P)):
            keep[name] = nc.dram_tensor(name, (rows, D), F32).ap()
        adj_in = [whole.enter_context(nc.semaphore(f"adj_in{k}")) for k in range(4)]
        with ExitStack() as part:
            layer0 = buffers(part, V=([P, NT, H, VW],), F1=([P, H, N],), F2=([P, 2, NT, H],), ADJ0=([P, 2, N],))
            layer0["adj_in"] = adj_in[:2]
            layer0_prepare(nc, io, {**keep, **layer0})
            layer0_attention(nc, io, {**keep, **layer0})
        with ExitStack() as part:
            moe = buffers(part, XF=([P, NT, D],), POSI=([P, TOPK * NT], U32), GW=([P, TOPK, NT],),
                          GD=([P, NT, E],), TE=([1, XTILES], I32))
            with ExitStack() as weights:
                moe.update(buffers(weights, W1=([P, E, KD, F],), W2=([P, E, FB, D],)),
                           w_in=weights.enter_context(nc.semaphore("expert_weights_in")))
                moe_route(nc, io, keep, moe)
                moe_experts(nc, io, keep, moe)
            moe_combine(nc, io, keep, moe)
        with ExitStack() as part:
            layer1 = buffers(part, V1=([P, NT, H, VW],), QT=([P, H, NT * P], F16), KH=([P, H, N], F16),
                             KL=([P, H, N], F16), ADJ1=([P, 2, N],))
            layer1["adj_in"] = adj_in[2:]
            layer1_prepare(nc, io, {**keep, "V": layer1["V1"]}, layer1)
            layer1_attention(nc, io, {**keep, "V": layer1["V1"]}, layer1)
        layer1_project(nc, io, keep)
        layer1_ffn(nc, io, keep)


_INS = ["x", "adj", "L0_gnn_weight", "L0_gnn_weight_u", "L0_gnn_weight_v", "L0_gnn_bias", "L0_gnn_proj_w",
        "L0_gnn_proj_b", "L0_ffn_gate_w", "L0_ffn_gate_b", "L0_ffn_w1", "L0_ffn_b1", "L0_ffn_w2", "L0_ffn_b2",
        "L0_ffn_gamma", "L0_ffn_beta", "L1_gnn_Wqkv", "L1_gnn_bqkv", "L1_gnn_Wout", "L1_gnn_bout",
        "L1_gnn_graph_bias", "L1_ffn_ln_w", "L1_ffn_ln_b", "L1_ffn_W", "L1_ffn_b"]


def kernel(**inputs):
    import numpy as _np
    import concourse.bacc as _bacc
    from concourse import mybir as _mybir
    from concourse.bass_utils import run_bass_kernel_spmd as _run

    nc = _bacc.Bacc("TRN2", target_bir_lowering=False, num_devices=1)
    arrays, io = {}, {}
    for name in _INS:
        a = _np.ascontiguousarray(inputs[name])
        arrays[f"in_{name}"] = a
        io[name] = nc.dram_tensor(f"in_{name}", a.shape, _mybir.dt.from_np(a.dtype), kind="ExternalInput").ap()
    io["out"] = nc.dram_tensor("out", (N, D), _mybir.dt.float32, kind="ExternalOutput").ap()
    build(nc, io)
    r = _run(nc, [arrays], core_ids=[0])
    return r.results[0]["out"]
```
